# Optimizing a Trainium2 kernel written in Bass

```python
import numpy as np
import jax
import jax.numpy as jnp

def _softmax(x, axis=-1):
    return jax.nn.softmax(x, axis=axis)

def _gelu(x):
    return jax.nn.gelu(x, approximate=True)

def _silu(x):
    return jax.nn.silu(x)

def _sigmoid(x):
    return jax.nn.sigmoid(x)

def _layernorm(x, axis=-1, eps=1e-05):
    m = jnp.mean(x, axis=axis, keepdims=True)
    v = jnp.var(x, axis=axis, keepdims=True)
    return (x - m) / jnp.sqrt(v + eps)

def _scatter_add(tgt, idx, src, axis=0):
    return tgt.at[idx].add(src)

def _segment_sum(src, seg, n):
    return jax.ops.segment_sum(src, seg, n)
kernel_name = 'mk_adj_resnorm_d2_adj_r2_da5f37'

def setup_inputs(seed: int=0):
    np.random.seed(seed)
    _w = jnp.asarray

    def _rec_inputs():
        import jax
        import jax.numpy as jnp
        _gk = jax.random.key(seed)
        x = -0.001003 + 1 * jax.random.normal(jax.random.fold_in(_gk, 1), (6144, 128), jnp.float32)
        _a = jax.random.bernoulli(jax.random.fold_in(_gk, 2), 0.000651042, (6144, 6144))
        _a = jnp.logical_or(_a, jnp.eye(6144, dtype=bool))
        _af = _a.astype(jnp.float32)
        _af = _af * jax.random.uniform(jax.random.fold_in(_gk, 3), (6144, 6144), jnp.float32, 0.05, 1)
        adj = _af
        return (x, adj)
    x, adj = _rec_inputs()

    def _L0_gnn_setup():
        import jax, jax.numpy as jnp
        import numpy as np
        TAU = 1.0
        EPS = 1e-10
        LN_EPS = 1e-05

        def _layernorm(x, g, b):
            m = jnp.mean(x, axis=-1, keepdims=True)
            v = jnp.mean((x - m) ** 2, axis=-1, keepdims=True)
            return (x - m) * jax.lax.rsqrt(v + LN_EPS) * g + b
        key = jax.random.key(seed)
        N, D = (6144, 128)
        ks = jax.random.split(key, 12)
        s = 1.0 / np.sqrt(D)
        inp = {'x': jax.random.normal(ks[0], (N, D), jnp.float32), 'adj': jax.random.uniform(ks[1], (N, N), jnp.float32), 'u': jax.random.uniform(ks[2], (N, 2), jnp.float32), 'W1': jax.random.normal(ks[3], (D, D), jnp.float32) * s, 'b1': jnp.zeros((D,), jnp.float32), 'W2': jax.random.normal(ks[4], (D, D), jnp.float32) * s, 'b2': jnp.zeros((D,), jnp.float32), 'Wg': jax.random.normal(ks[5], (2 * D, D), jnp.float32) * s, 'bg': jnp.zeros((D,), jnp.float32), 'Wn': jax.random.normal(ks[6], (D, 2), jnp.float32) * s, 'bn': jnp.zeros((2,), jnp.float32), 'g_in': jnp.ones((D,), jnp.float32), 'b_in': jnp.zeros((D,), jnp.float32), 'g_out': jnp.ones((D,), jnp.float32), 'b_out': jnp.zeros((D,), jnp.float32)}
        return inp
    _L0_gnn_all = _L0_gnn_setup()
    _L0_gnn_in = {k: v for k, v in _L0_gnn_all.items() if k in ('u', 'W1', 'b1', 'W2', 'b2', 'Wg', 'bg', 'Wn', 'bn', 'g_in', 'b_in', 'g_out', 'b_out')}
    del _L0_gnn_all

    def _L1_gnn_setup():
        import jax, jax.numpy as jnp
        import numpy as np
        MIN_NORM = 1e-15
        BALL_EPS = 0.004
        C_IN = 1.0
        C_OUT = 1.0

        def _norm(x):
            return jnp.clip(jnp.linalg.norm(x, axis=-1, keepdims=True), MIN_NORM, None)

        def artanh(x):
            return jnp.arctanh(jnp.clip(x, -1.0 + 1e-07, 1.0 - 1e-07))

        def proj(x, c):
            norm = _norm(x)
            maxnorm = (1.0 - BALL_EPS) / jnp.sqrt(c)
            return jnp.where(norm > maxnorm, x / norm * maxnorm, x)

        def expmap0(u, c):
            sc = jnp.sqrt(c)
            un = _norm(u)
            return jnp.tanh(sc * un) * u / (sc * un)

        def logmap0(p, c):
            sc = jnp.sqrt(c)
            pn = _norm(p)
            return artanh(sc * pn) * p / (sc * pn)

        def mobius_add(x, y, c):
            x2 = jnp.sum(x * x, -1, keepdims=True)
            y2 = jnp.sum(y * y, -1, keepdims=True)
            xy = jnp.sum(x * y, -1, keepdims=True)
            num = (1 + 2 * c * xy + c * y2) * x + (1 - c * x2) * y
            denom = 1 + 2 * c * xy + c * c * x2 * y2
            return num / jnp.clip(denom, MIN_NORM, None)

        def mobius_matvec(m, x, c):
            sc = jnp.sqrt(c)
            xn = _norm(x)
            mx = x @ m.T
            mxn = _norm(mx)
            res = jnp.tanh(mxn / xn * artanh(sc * xn)) * mx / (mxn * sc)
            zero_rows = jnp.all(mx == 0, axis=-1, keepdims=True)
            return jnp.where(zero_rows, jnp.zeros_like(res), res)
        key = jax.random.key(seed)
        k1, k2, k3, k4 = jax.random.split(key, 4)
        N, din, dout = (8192, 128, 128)
        x = jax.random.normal(k1, (N, din), dtype=jnp.float32) * 0.01
        adj = jax.random.uniform(k2, (N, N), dtype=jnp.float32)
        adj = adj / jnp.sum(adj, axis=-1, keepdims=True)
        bound = math_bound = float(np.sqrt(2.0) * np.sqrt(6.0 / (din + dout)))
        weight = jax.random.uniform(k3, (dout, din), dtype=jnp.float32, minval=-bound, maxval=bound)
        bias = jax.random.normal(k4, (dout,), dtype=jnp.float32) * 0.01
        return {'x': x, 'adj': adj, 'weight': weight, 'bias': bias}
    _L1_gnn_all = _L1_gnn_setup()
    _L1_gnn_in = {k: v for k, v in _L1_gnn_all.items() if k in ('weight', 'bias')}
    del _L1_gnn_all
    return {'x': x, 'adj': adj, 'L0_gnn_u': _L0_gnn_in['u'], 'L0_gnn_W1': _L0_gnn_in['W1'], 'L0_gnn_b1': _L0_gnn_in['b1'], 'L0_gnn_W2': _L0_gnn_in['W2'], 'L0_gnn_b2': _L0_gnn_in['b2'], 'L0_gnn_Wg': _L0_gnn_in['Wg'], 'L0_gnn_bg': _L0_gnn_in['bg'], 'L0_gnn_Wn': _L0_gnn_in['Wn'], 'L0_gnn_bn': _L0_gnn_in['bn'], 'L0_gnn_g_in': _L0_gnn_in['g_in'], 'L0_gnn_b_in': _L0_gnn_in['b_in'], 'L0_gnn_g_out': _L0_gnn_in['g_out'], 'L0_gnn_b_out': _L0_gnn_in['b_out'], 'L1_gnn_weight': _L1_gnn_in['weight'], 'L1_gnn_bias': _L1_gnn_in['bias']}

def reference(x, adj, L0_gnn_u, L0_gnn_W1, L0_gnn_b1, L0_gnn_W2, L0_gnn_b2, L0_gnn_Wg, L0_gnn_bg, L0_gnn_Wn, L0_gnn_bn, L0_gnn_g_in, L0_gnn_b_in, L0_gnn_g_out, L0_gnn_b_out, L1_gnn_weight, L1_gnn_bias):
    import jax
    import jax.numpy as jnp

    def _L0_gnn_ref(x, adj, u, W1, b1, W2, b2, Wg, bg, Wn, bn, g_in, b_in, g_out, b_out):
        import jax, jax.numpy as jnp
        import numpy as np
        TAU = 1.0
        EPS = 1e-10
        LN_EPS = 1e-05

        def _layernorm(x, g, b):
            m = jnp.mean(x, axis=-1, keepdims=True)
            v = jnp.mean((x - m) ** 2, axis=-1, keepdims=True)
            return (x - m) * jax.lax.rsqrt(v + LN_EPS) * g + b
        residual = x
        x_norm = _layernorm(x, g_in, b_in)
        logits = x_norm @ Wn + bn
        gumbel = -jnp.log(-jnp.log(jnp.clip(u, EPS, 1.0)) + EPS)
        y_soft = jax.nn.softmax((logits + gumbel) / TAU, axis=-1)
        hard = jax.nn.one_hot(jnp.argmax(y_soft, axis=-1), 2, dtype=y_soft.dtype)
        y = hard + y_soft - jax.lax.stop_gradient(y_soft)
        gate = y[:, 1]
        sel_adj = adj * gate[:, None] * gate[None, :]
        view1 = x_norm
        view2 = sel_adj @ x_norm
        fusion_gate = jax.nn.sigmoid(jnp.concatenate([view1, view2], axis=-1) @ Wg + bg)
        fused = fusion_gate * (view1 @ W1 + b1) + (1.0 - fusion_gate) * (view2 @ W2 + b2)
        return _layernorm(fused + residual, g_out, b_out)

    def _L1_gnn_ref(x, adj, weight, bias):
        import jax, jax.numpy as jnp
        import numpy as np
        MIN_NORM = 1e-15
        BALL_EPS = 0.004
        C_IN = 1.0
        C_OUT = 1.0

        def _norm(x):
            return jnp.clip(jnp.linalg.norm(x, axis=-1, keepdims=True), MIN_NORM, None)

        def artanh(x):
            return jnp.arctanh(jnp.clip(x, -1.0 + 1e-07, 1.0 - 1e-07))

        def proj(x, c):
            norm = _norm(x)
            maxnorm = (1.0 - BALL_EPS) / jnp.sqrt(c)
            return jnp.where(norm > maxnorm, x / norm * maxnorm, x)

        def expmap0(u, c):
            sc = jnp.sqrt(c)
            un = _norm(u)
            return jnp.tanh(sc * un) * u / (sc * un)

        def logmap0(p, c):
            sc = jnp.sqrt(c)
            pn = _norm(p)
            return artanh(sc * pn) * p / (sc * pn)

        def mobius_add(x, y, c):
            x2 = jnp.sum(x * x, -1, keepdims=True)
            y2 = jnp.sum(y * y, -1, keepdims=True)
            xy = jnp.sum(x * y, -1, keepdims=True)
            num = (1 + 2 * c * xy + c * y2) * x + (1 - c * x2) * y
            denom = 1 + 2 * c * xy + c * c * x2 * y2
            return num / jnp.clip(denom, MIN_NORM, None)

        def mobius_matvec(m, x, c):
            sc = jnp.sqrt(c)
            xn = _norm(x)
            mx = x @ m.T
            mxn = _norm(mx)
            res = jnp.tanh(mxn / xn * artanh(sc * xn)) * mx / (mxn * sc)
            zero_rows = jnp.all(mx == 0, axis=-1, keepdims=True)
            return jnp.where(zero_rows, jnp.zeros_like(res), res)
        mv = mobius_matvec(weight, x, C_IN)
        res = proj(mv, C_IN)
        hyp_bias = proj(expmap0(bias[None, :], C_IN), C_IN)
        h = proj(mobius_add(res, hyp_bias, C_IN), C_IN)
        xt = logmap0(h, C_IN)
        support_t = adj @ xt
        h = proj(expmap0(support_t, C_IN), C_IN)
        xt = jax.nn.relu(logmap0(h, C_IN))
        h = proj(expmap0(xt, C_OUT), C_OUT)
        return h
    x = _layernorm(x + _L0_gnn_ref(x, adj, L0_gnn_u, L0_gnn_W1, L0_gnn_b1, L0_gnn_W2, L0_gnn_b2, L0_gnn_Wg, L0_gnn_bg, L0_gnn_Wn, L0_gnn_bn, L0_gnn_g_in, L0_gnn_b_in, L0_gnn_g_out, L0_gnn_b_out), axis=-1)
    x = _layernorm(x + _L1_gnn_ref(x, adj, L1_gnn_weight, L1_gnn_bias), axis=-1)
    return x

_drawn_inputs = setup_inputs


def setup_inputs(seed=0):
    import zlib

    import numpy as np

    out = dict(_drawn_inputs(seed))
    spreads = {'L0_gnn_b1': (0.0, 0.304),
     'L0_gnn_b2': (0.0, 0.342),
     'L0_gnn_bg': (0.0, 0.711),
     'L0_gnn_bn': (0.0, 0.1),
     'L0_gnn_g_in': (1.0, 0.2),
     'L0_gnn_b_in': (0.0, 0.1),
     'L0_gnn_g_out': (1.0, 0.2),
     'L0_gnn_b_out': (0.0, 0.1)}
    factors = {'L1_gnn_bias': 8.0}
    for name, (base, spread) in spreads.items():
        noise = np.random.default_rng([zlib.crc32(name.encode()), seed]).standard_normal(out[name].shape)
        drawn = base * np.exp(spread * noise) if base else spread * noise
        out[name] = jnp.asarray(drawn.astype(out[name].dtype))
    for name, factor in factors.items():
        out[name] = (out[name] * factor).astype(out[name].dtype)
    return out
```

```python
from contextlib import ExitStack

import concourse.bass as bass
from concourse import mybir

F32 = mybir.dt.float32
F32R = mybir.dt.float32r
BF16 = mybir.dt.bfloat16
ALU = mybir.AluOpType
ACT = mybir.ActivationFunctionType

P = 128
BLK = 4
CW = BLK * P
GW = BLK * CW
RING = 4
LN_EPS = 1e-5
U_EPS = 1e-10
MIN_NORM = 1e-15
MIN_NORM2 = 1e-30
MAX_NORM = 0.996
ATANH_CLIP = 0.9999998807907104
ATANH_MAX_NORM = 3.1063027
SERIES_BELOW2 = 0.0025


def low(c):
    return RING * ((c - 1) // RING) if c >= 1 else 0


def bands(nch):
    out = []
    for c in range(1, nch):
        if out and out[-1][2] == low(c):
            out[-1][1] = c + 1
        else:
            out.append([c, c + 1, low(c)])
    return [tuple(b) for b in out]


def slot_of(k, groups):
    return min(groups - 1, max(1, (k * groups + 6) // 12))


def build(nc, x, adjT, u, w1, b1, w2, b2, wg, bg, wn, bn, g_in, b_in, g_out, b_out, w_hyp, b_hyp, out):
    N = x.shape[0] * x.shape[1] // P
    NCH = N // CW
    NB = N // P
    N1 = NCH * NCH
    assert NCH % RING == 0

    with ExitStack() as ctx:
        def sb(name, shape, dt=F32):
            return ctx.enter_context(nc.sbuf_tensor(name, shape, dt))

        def sem(name):
            return ctx.enter_context(nc.semaphore(name))

        A = sb("A", [P, RING, GW])
        AH = sb("AH", [P, 2, GW], F32R)
        AL = sb("AL", [P, 2, GW], F32R)
        XN = A[:, :, :].rearrange("p r n -> p (r n)")
        XGH = sb("XGH", [P, N], F32R)
        XGL = sb("XGL", [P, N], F32R)
        XTH = sb("XTH", [P, N], F32R)
        XTL = sb("XTL", [P, N], F32R)
        first_low = min([c for c in range(NCH) if low(c)] or [NCH])
        PART = sb("PART", [P, NCH - first_low + 1, CW])
        XR = sb("XR", [P, CW])
        XNT = sb("XNT", [P, CW])
        GB = sb("GB", [P, CW])
        TH = sb("TH", [P, CW])
        FU = sb("FU", [P, CW])
        X1 = sb("X1", [P, CW])
        X1T = sb("X1T", [P, CW])
        HY = sb("HY", [P, CW])
        JUNK = sb("JUNK", [P, CW])
        ident = sb("ident", [P, P])
        RX = sb("RX", [P, 2 * P])
        RS = sb("RS", [P, 3 * P])
        RM = sb("RM", [P, P + 1])
        WH = sb("WH", [P, P])
        WN = sb("WN", [P, 2])
        GIN = sb("GIN", [P, P])
        BIN = sb("BIN", [P, P])
        GOUT = sb("GOUT", [P, P])
        BOUT = sb("BOUT", [P, P])
        HB = sb("HB", [P, P])
        HBC = sb("HBC", [P, 1])
        BNB = sb("BNB", [P, 2])
        B3 = sb("B3", [P, 3 * P])
        BP = sb("BP", [P, 3 * P], BF16)
        BR = sb("BR", [P, 3 * P], BF16)
        ones = sb("ones", [P, P], BF16)
        NHALF = sb("NHALF", [P, NB])
        NEG1 = sb("NEG1", [P, BLK])
        U = sb("U", [P, NB * 2])
        LG = sb("LG", [P, NB, 2])
        TOP = sb("TOP", [P, NB])
        SM = sb("SM", [P, NB])
        GATE = sb("GATE", [P, NB])
        GATET = sb("GATET", [NB, P])
        BS = sb("BS", [P, BLK, 6])
        MV = sb("MV", [P, BLK, 2])
        MV2 = sb("MV2", [P, BLK, 2])
        small = {n: sb("r_" + n, [P, BLK]) for n in (
            "v", "rs", "rs2", "n2", "inv", "t", "tc", "la", "lb", "ser", "mask", "fx", "m2", "pxy", "minv", "q",
            "tq", "rsc", "x2", "xy", "a", "b", "den", "alpha", "beta", "h2", "kap", "s2", "r2", "w", "nr")}
        y2 = sb("y2", [P, 1])
        hbs = sb("hbs", [P, 5])

        ACC = ctx.enter_context(nc.psum_tensor("ACC", [P, 4 * CW], F32))
        E = ctx.enter_context(nc.psum_tensor("E", [P, 4, CW], F32))

        xnt_dram = nc.dram_tensor("xnt_scratch", [NCH * P, CW], F32).ap()
        gate_dram = nc.dram_tensor("gate_scratch", [NCH, CW], F32).ap()
        x1_dram = nc.dram_tensor("x1_scratch", [NCH * P, CW], F32).ap()

        S = {}
        for name in (
                "act_link", "alphabeta", "bias_ready", "centered", "coef", "const", "dve_link",
                "epi_in", "gate_arg", "gate_exp", "gate_rows", "gate_stored", "gate_tr", "gated",
                "gates", "gum1", "gum2", "h", "hb_norm", "hb_ready", "hb_sq", "hb_tanh", "hi",
                "ident_ready", "kap", "l0_mm", "ld0", "ld1", "ld2", "ld3", "ln1", "ln2", "lo", "mx",
                "n3", "part_saved", "pool_link", "pre_logit", "pre_rs", "pre_stats", "pre_tr",
                "pre_xn", "pre_xt", "pre_z", "q", "res", "res_stored", "rm_psum", "rm_ready", "rs1",
                "rs2", "rs3", "s1_gated", "s2_taken", "s2_tr", "scaled", "sq1", "sq2", "sq3",
                "stats1", "stats2", "stats3", "tanh", "tc1", "tc2", "th3", "tq", "urow", "used",
                "vecs", "weights", "wt_scaled", "x1_back", "x1_ready", "x1_stored", "x1_tr", "x1t",
                "xb", "xgh", "xgl", "xin0", "xin1", "xnt_stored0", "xn_kept", "xnt_stored1", "xth", "xtl",
                "y2_ready"):
            S[name] = sem("s_" + name)

        block = ctx.enter_context(nc.Block())

        class Link:

            def __init__(self, eng, s, base=0, nop=False):
                self.eng, self.s, self.base, self.nop, self.n = eng, s, base, nop, 0

            def __call__(self, ins):
                self.n += 1
                ins.then_inc(self.s, 1)
                self.eng.wait_ge(self.s, self.base + self.n)
                if self.nop:
                    self.eng.nop(nofuse=True)

        def wait_n(eng, name, value):
            if not (isinstance(value, int) and value <= 0):
                eng.wait_ge(S[name], value)

        def b4(ap):
            return ap.rearrange("p (o d) -> p o d", o=1).to_broadcast([P, BLK, P])

        def v4(ap):
            return ap.rearrange("p (b d) -> p b d", b=BLK)

        def blk(t):
            return slice(t * P, (t + 1) * P)

        def phase2_base():
            base, n = {0: N1}, N1 + NCH
            for lo_c, hi_c, lw in bands(NCH):
                base[lo_c] = n
                n += (hi_c - lo_c) * (NCH - lw)
            return base
        BASE2 = phase2_base()
        TOTAL = N1 + sum(NCH - low(c) for c in range(NCH))

        def steps(eng, body):
            body(1, 0, 0, 0)
            for c0, c1, lw in bands(NCH):
                with eng.Fori(c0, c1) as c:
                    body(1, c, lw, NCH * c)
            body(2, 0, 0, N1)
            for c0, c1, lw in bands(NCH):
                with eng.Fori(c0, c1) as c:
                    body(2, c, lw, BASE2[c0] + (NCH - lw) * (c - c0))

        def turns(n0):
            return n0 // RING if isinstance(n0, int) else n0 >> 2

        def at1(k):
            return slot_of(k, NCH)
        K_GATED, K_TANH, K_PRE, K_X1, K_X1T, K_SQ1, K_TQ, K_H, K_LN2, K_XT = (
            at1(k) for k in (1, 3, 4, 5, 6, 7, 8, 9, 10, 11))

        @block.sync
        def _(sp):
            sp.dma_start(RX[:, 0:P], wg[0:P, :]).then_inc(S["weights"], 16)
            sp.dma_start(RX[:, P:2 * P], w1).then_inc(S["weights"], 16)
            sp.dma_start(RS[:, 0:P], wg[P:2 * P, :]).then_inc(S["weights"], 16)
            sp.dma_start(RS[:, P:2 * P], w2).then_inc(S["weights"], 16)
            sp.dma_start(RS[:, 2 * P:3 * P], w2).then_inc(S["weights"], 16)
            sp.dma_start(WH[:, :], w_hyp).then_inc(S["weights"], 16)
            sp.dma_start(WN[:, :], wn).then_inc(S["weights"], 16)
            for t, v in ((GIN[:, :], g_in), (BIN[:, :], b_in), (GOUT[:, :], g_out), (BOUT[:, :], b_out),
                         (HB[:, :], b_hyp), (B3[:, 0:P], bg), (B3[:, P:2 * P], b1), (B3[:, 2 * P:3 * P], b2),
                         (BNB[:, :], bn)):
                sp.dma_start(t, v.partition_broadcast(P)).then_inc(S["vecs"], 16)
            sp.dma_start(HBC[:, :], b_hyp.rearrange("(p o) -> p o", o=1)).then_inc(S["vecs"], 16)
            sp.dma_start(U[:, :], u).then_inc(S["urow"], 16)

            def load_x(h):
                for r, buf in enumerate((XR, FU)):
                    wait_n(sp, "pre_z", 2 * h)
                    sp.dma_start(buf[:, :], x[bass.ds((2 * h + r) * P, P), :]).then_inc(S[f"xin{r}"], 16)

            def store_xnt(h):
                for r, buf in enumerate((XNT, X1T)):
                    sp.wait_ge(S["pre_xt"], 2 * h + r + 1)
                    sp.dma_start(xnt_dram[bass.ds((2 * h + r) * P, P), :],
                                 buf[:, :]).then_inc(S[f"xnt_stored{r}"], 16)
            load_x(0)
            with sp.Fori(0, NCH // 2 - 1) as h:
                load_x(h + 1)
                store_xnt(h)
            store_xnt(NCH // 2 - 1)
            sp.wait_ge(S["gate_rows"], 1)
            sp.dma_start(gate_dram.rearrange("c (t p) -> (c t) p", p=P), GATET[:, :]).then_inc(S["gate_stored"], 16)

            def load(phase, c, q, n0, q0):
                if phase == 1 and isinstance(c, int):
                    if q < RING:
                        sp.wait_ge(S["xgl"], min(NCH, RING * (q + 1)))
                    else:
                        sp.wait_ge(S["lo"], q - RING + 1)
                else:
                    sp.wait_ge(S["lo"], n0 + (q - q0) - RING + 1)
                sp.dma_start(A[:, q % RING, :],
                             adjT[bass.ds((c * NCH + q) * P, P), :]).then_inc(S[f"ld{q % RING}"], 16)

            def body(phase, c, lw, n0):
                q0 = lw if phase == 2 else 0
                for q in range(q0, NCH):
                    if phase == 1 and q == NCH - 2:
                        if isinstance(c, int):
                            sp.wait_ge(S["gate_stored"], 16)
                            sp.wait_ge(S["xnt_stored0"], 16 * (NCH // 2))
                            sp.wait_ge(S["xnt_stored1"], 16 * (NCH // 2))
                        wait_n(sp, "stats2", c)
                        wait_n(sp, "l0_mm", c)
                        sp.dma_start(XR[:, :], x[bass.ds(c * P, P), :]).then_inc(S["epi_in"], 16)
                        sp.dma_start(XNT[:, :], xnt_dram[bass.ds(c * P, P), :]).then_inc(S["epi_in"], 16)
                        sp.dma_start(GB[:, :], gate_dram[bass.ds(c, 1), :].partition_broadcast(P)
                                     ).then_inc(S["epi_in"], 16)
                    load(phase, c, q, n0, q0)
            steps(sp, body)

        @block.gpsimd
        def _(pool):
            g = nc.gpsimd
            r = {k: v[:, :] for k, v in small.items()}
            g.memset(ident[:, :], 0.0).then_inc(S["ident_ready"], 1)
            g.memset(ones[:, :], 1.0)
            g.memset(NHALF[:, :], -0.5)
            g.memset(NEG1[:, :], -1.0)
            g.memset(BP[:, :], 0.0).then_inc(S["const"], 1)
            pool.wait_ge(S["ident_ready"], 1)
            g.affine_select(out=ident[:, :], in_=ident[:, :], compare_op=ALU.not_equal, fill=1.0, base=0,
                            pattern=[[-1, P]], channel_multiplier=1).then_inc(S["ident_ready"], 1)
            SETUP = 5
            link = Link(pool, S["pool_link"])
            pool.wait_ge(S["vecs"], 160)
            pool.wait_ge(S["const"], 1)
            pool.wait_ge(S["hb_sq"], 1)
            pool.nop(nofuse=True)
            link(g.tensor_scalar(hbs[:, 1:2], hbs[:, 0:1], MIN_NORM2, None, ALU.max))
            link(g.tensor_tensor(hbs[:, 2:3], hbs[:, 1:2], NHALF[:, 0:1], ALU.pow))
            g.tensor_tensor(hbs[:, 3:4], hbs[:, 1:2], hbs[:, 2:3], ALU.mult).then_inc(S["hb_norm"], 1)
            pool.wait_ge(S["hb_tanh"], 1)
            pool.nop(nofuse=True)
            link(g.tensor_scalar(hbs[:, 4:5], hbs[:, 4:5], MAX_NORM, None, ALU.min))
            link(g.tensor_tensor(hbs[:, 4:5], hbs[:, 4:5], hbs[:, 2:3], ALU.mult))
            link(g.tensor_tensor(HB[:, :], HB[:, :], hbs[:, 4:5].to_broadcast([P, P]), ALU.mult))
            g.tensor_tensor(HBC[:, :], HBC[:, :], hbs[:, 4:5], ALU.mult).then_inc(S["hb_ready"], 1)
            assert link.n == SETUP
            K = 2
            def prelude(h):
                link = Link(pool, S["pool_link"], SETUP + 2 * K * h, nop=True)
                for k in range(2):
                    q = 2 * h + k
                    pool.wait_ge(S["pre_stats"], q + 1)
                    pool.nop(nofuse=True)
                    link(g.tensor_scalar(r["v"], MV[:, :, 1], LN_EPS, None, ALU.add))
                    g.tensor_tensor(r["rs"], r["v"], NHALF[:, 0:BLK], ALU.pow).then_inc(S["pre_rs"], 1)
                    pool.wait_ge(S["pre_z"], q + 1)
                    link(g.tensor_tensor(v4(HY[:, :]), v4(TH[:, :]), b4(GIN[:, :]), ALU.mult))
                    wait_n(pool, "pre_tr", 2 * h)
                    wait_n(pool, "xn_kept", 2 * h)
                    g.tensor_tensor(v4(PART[:, 1 + k, :]), v4(HY[:, :]), b4(BIN[:, :]),
                                    ALU.add).then_inc(S["pre_xn"], 1)
                assert link.n == 2 * K
            prelude(0)
            with pool.Fori(1, NCH // 2) as h:
                prelude(h)

            def atanh_ratio(link, e, n2, clip, tc_sem, ln_sem, k_out):
                link(g.tensor_scalar(r["n2"], n2, MIN_NORM2, None, ALU.max))
                link(g.tensor_tensor(r["inv"], r["n2"], NHALF[:, 0:BLK], ALU.pow))
                link(g.tensor_tensor(r["t"], r["n2"], r["inv"], ALU.mult))
                g.tensor_scalar(r["tc"], r["t"], clip, None, ALU.min).then_inc(S[tc_sem], 1)
                link(g.tensor_scalar(r["ser"], r["n2"], 0.2, 1.0 / 3.0, ALU.mult, ALU.add))
                link(g.tensor_tensor(r["ser"], r["ser"], r["n2"], ALU.mult))
                link(g.tensor_scalar(r["ser"], r["ser"], 1.0, None, ALU.add))
                link(g.tensor_scalar(r["mask"], r["n2"], SERIES_BELOW2, None, ALU.is_lt))
                pool.wait_ge(S[ln_sem], e + 1)
                link(g.tensor_tensor(r["la"], r["la"], r["lb"], ALU.subtract))
                link(g.tensor_tensor(r["la"], r["la"], r["inv"], ALU.mult))
                link(g.tensor_scalar(r["la"], r["la"], 0.5, None, ALU.mult))
                link(g.tensor_tensor(r["ser"], r["ser"], r["la"], ALU.subtract))
                link(g.tensor_tensor(r["ser"], r["ser"], r["mask"], ALU.mult))
                return g.tensor_tensor(k_out, r["ser"], r["la"], ALU.add)

            BASE1 = SETUP + K * NCH
            K1 = 47

            def chunk_end(e):
                link = Link(pool, S["pool_link"], BASE1 + K1 * e, nop=True)
                pool.wait_ge(S["stats1"], e + 1)
                pool.nop(nofuse=True)
                link(g.tensor_scalar(r["v"], MV[:, :, 1], LN_EPS, None, ALU.add))
                g.tensor_tensor(r["rs"], r["v"], NHALF[:, 0:BLK], ALU.pow).then_inc(S["rs1"], 1)
                g.tensor_tensor(v4(XR[:, :]), v4(XR[:, :]), b4(BOUT[:, :]), ALU.add).then_inc(S["xb"], 1)
                pool.wait_ge(S["stats2"], e + 1)
                pool.nop(nofuse=True)
                link(g.tensor_scalar(r["v"], MV2[:, :, 1], LN_EPS, None, ALU.add))
                g.tensor_tensor(r["rs2"], r["v"], NHALF[:, 0:BLK], ALU.pow).then_inc(S["rs2"], 1)
                pool.wait_ge(S["rs2"], e + 1)
                link(g.tensor_tensor(r["a"], r["rs2"], r["rs2"], ALU.mult))
                link(g.tensor_tensor(r["a"], r["a"], MV2[:, :, 1], ALU.mult))
                link(g.tensor_scalar(r["a"], r["a"], float(P), None, ALU.mult))
                link(atanh_ratio(link, e, r["a"], ATANH_CLIP, "tc1", "ln1", r["fx"]))
                pool.wait_ge(S["x1_ready"], e + 1)
                pool.nop(nofuse=True)
                pool.dma_start(x1_dram[bass.ds(e * P, P), :], X1[:, :]).then_inc(S["x1_stored"], 16)
                pool.wait_ge(S["sq1"], e + 1)
                pool.nop(nofuse=True)
                link(g.tensor_scalar(r["n2"], r["m2"], MIN_NORM2, None, ALU.max))
                link(g.tensor_tensor(r["minv"], r["n2"], NHALF[:, 0:BLK], ALU.pow))
                link(g.tensor_tensor(r["t"], r["n2"], r["minv"], ALU.mult))
                g.tensor_tensor(r["q"], r["t"], r["fx"], ALU.mult).then_inc(S["q"], 1)
                pool.wait_ge(S["tq"], e + 1)
                pool.nop(nofuse=True)
                link(g.tensor_scalar(r["tq"], r["tq"], MAX_NORM, None, ALU.min))
                link(g.tensor_tensor(r["rsc"], r["tq"], r["minv"], ALU.mult))
                link(g.tensor_tensor(r["x2"], r["rsc"], r["rsc"], ALU.mult))
                link(g.tensor_tensor(r["x2"], r["x2"], r["m2"], ALU.mult))
                link(g.tensor_tensor(r["xy"], r["rsc"], r["pxy"], ALU.mult))
                link(g.tensor_scalar(r["xy"], r["xy"], 2.0, 1.0, ALU.mult, ALU.add))
                link(g.tensor_tensor(r["a"], r["xy"], y2[:, 0:1].to_broadcast([P, BLK]), ALU.add))
                link(g.tensor_scalar(r["b"], r["x2"], -1.0, 1.0, ALU.mult, ALU.add))
                link(g.tensor_tensor(r["den"], r["x2"], y2[:, 0:1].to_broadcast([P, BLK]), ALU.mult))
                link(g.tensor_tensor(r["den"], r["den"], r["xy"], ALU.add))
                link(g.tensor_scalar(r["den"], r["den"], MIN_NORM, None, ALU.max))
                link(g.tensor_tensor(r["den"], r["den"], NEG1[:, :], ALU.pow))
                link(g.tensor_tensor(r["beta"], r["b"], r["den"], ALU.mult))
                link(g.tensor_tensor(r["a"], r["a"], r["den"], ALU.mult))
                g.tensor_tensor(r["alpha"], r["a"], r["rsc"], ALU.mult).then_inc(S["alphabeta"], 1)
                pool.wait_ge(S["sq2"], e + 1)
                pool.nop(nofuse=True)
                atanh_ratio(link, e, r["h2"], MAX_NORM, "tc2", "ln2", r["kap"]).then_inc(S["kap"], 1)
                pool.wait_ge(S["x1_stored"], 16 * (e + 1))
                assert link.n == K1, link.n

            BASE3 = BASE1 + K1 * NCH
            K3 = 10

            def result(e):
                link = Link(pool, S["pool_link"], BASE3 + K3 * e, nop=True)
                pool.dma_start(XR[:, :], x1_dram[bass.ds(e * P, P), :]).then_inc(S["x1_back"], 16)
                pool.wait_ge(S["sq3"], e + 1)
                pool.nop(nofuse=True)
                link(g.tensor_scalar(r["s2"], r["s2"], MIN_NORM2, None, ALU.max))
                link(g.tensor_tensor(r["w"], r["s2"], NHALF[:, 0:BLK], ALU.pow))
                link(g.tensor_scalar(r["w"], r["w"], ATANH_MAX_NORM, None, ALU.mult))
                link(g.tensor_scalar(r["w"], r["w"], 1.0, None, ALU.min))
                link(g.tensor_scalar(r["r2"], r["r2"], MIN_NORM2, None, ALU.max))
                link(g.tensor_tensor(r["nr"], r["r2"], NHALF[:, 0:BLK], ALU.pow))
                link(g.tensor_tensor(r["nr"], r["nr"], r["r2"], ALU.mult))
                link(g.tensor_tensor(r["nr"], r["nr"], r["w"], ALU.mult))
                g.tensor_scalar(r["t"], r["nr"], MIN_NORM, None, ALU.max).then_inc(S["n3"], 1)
                pool.wait_ge(S["n3"], e + 1)
                link(g.tensor_tensor(r["inv"], r["t"], NEG1[:, :], ALU.pow))
                pool.wait_ge(S["th3"], e + 1)
                pool.nop(nofuse=True)
                link(g.tensor_scalar(r["tq"], r["tq"], MAX_NORM, None, ALU.min))
                g.tensor_tensor(r["inv"], r["inv"], r["tq"], ALU.mult).then_inc(S["coef"], 1)
                pool.wait_ge(S["coef"], 2 * e + 1)
                g.tensor_tensor(r["kap"], r["inv"], r["w"], ALU.mult).then_inc(S["coef"], 1)
                pool.wait_ge(S["stats3"], e + 1)
                pool.nop(nofuse=True)
                g.tensor_scalar(r["v"], MV[:, :, 1], LN_EPS, None, ALU.add).then_inc(S["rs3"], 1)
                pool.wait_ge(S["rs3"], 2 * e + 1)
                g.tensor_tensor(r["rs"], r["v"], NHALF[:, 0:BLK], ALU.pow).then_inc(S["rs3"], 1)
                pool.wait_ge(S["res"], e + 1)
                pool.nop(nofuse=True)
                pool.dma_start(out[bass.ds(e * P, P), :], X1[:, :]).then_inc(S["res_stored"], 16)
                pool.wait_ge(S["res_stored"], 16 * (e + 1))
                assert link.n == K3, link.n

            pool.wait_ge(S["y2_ready"], 1)
            with pool.Fori(0, NCH) as e:
                chunk_end(e)
            with pool.Fori(0, NCH) as e:
                result(e)

        @block.scalar
        def _(act):
            a = nc.scalar
            r = {k: v[:, :] for k, v in small.items()}
            act.wait_ge(S["gum1"], 1)
            a.activation(U[:, :], U[:, :], ACT.Ln).then_inc(S["gum2"], 1)
            act.wait_ge(S["gum1"], 2)
            a.activation(U[:, :], U[:, :], ACT.Ln).then_inc(S["gum2"], 1)
            act.wait_ge(S["vecs"], 160)
            a.activation(JUNK[:, 0:P], HB[:, :], ACT.Square, accum_out=hbs[:, 0:1]).then_inc(S["hb_sq"], 1)
            act.wait_ge(S["hb_norm"], 1)
            a.activation(hbs[:, 4:5], hbs[:, 3:4], ACT.Tanh).then_inc(S["hb_tanh"], 1)
            act.wait_ge(S["hb_ready"], 1)
            a.activation(JUNK[:, 0:P], HB[:, :], ACT.Square, accum_out=y2[:, 0:1]).then_inc(S["y2_ready"], 1)
            act.wait_ge(S["rm_psum"], 1)
            a.activation(RM[:, :], E[:, 3, 0:P + 1], ACT.Copy).then_inc(S["rm_ready"], 1)

            def prelude(h):
                for k, tbuf in enumerate((XNT, X1T)):
                    act.wait_ge(S["pre_xn"], 2 * h + k + 1)
                    a.activation(XN[:, bass.ds((2 * h + k) * CW, CW)], PART[:, 1 + k, :],
                                 ACT.Copy).then_inc(S["xn_kept"], 1)
                    act.wait_ge(S["pre_tr"], 2 * h + k + 1)
                    wait_n(act, f"xnt_stored{k}", 16 * h)
                    wait_n(act, "pre_logit", 2 * h)
                    a.activation(tbuf[:, :], E[:, 0, :], ACT.Copy).then_inc(S["pre_xt"], 1)
            prelude(0)
            with act.Fori(1, NCH // 2) as h:
                prelude(h)
            act.wait_ge(S["gate_arg"], 1)
            a.activation(LG[:, :, :], LG[:, :, :], ACT.Exp).then_inc(S["gate_exp"], 1)
            act.wait_ge(S["gate_tr"], 1)
            a.activation(GATET[:, :], E[0:NB, 2, 0:P], ACT.Copy).then_inc(S["gate_rows"], 1)
            with act.Fori(0, NCH) as q:
                act.wait_ge(S["gated"], q + 1)
                a.activation(XGH[:, bass.ds(q * CW, CW)], XN[:, bass.ds(q * CW, CW)], ACT.Copy).then_inc(S["xgh"], 1)

            def split_high(q, n0, q0):
                n = n0 + (q - q0)
                act.wait_ge(S[f"ld{q % RING}"], 16 * (turns(n0) + (q - q0) // RING + 1))
                if not (isinstance(n, int) and n < 2):
                    act.wait_ge(S["used"], n - 1)
                a.activation(AH[:, q % 2, :], A[:, q % RING, :], ACT.Copy).then_inc(S["hi"], 1)

            def chunk_end(q, e):
                if q == K_TANH:
                    act.wait_ge(S["l0_mm"], e + 1)
                    a.activation(v4(TH[:, :]), E[:, :, 0:P], ACT.Tanh, scale=0.5).then_inc(S["tanh"], 1)
                if q == K_X1T:
                    act.wait_ge(S["x1_tr"], e + 1)
                    a.activation(X1T[:, :], E[:, 0, :], ACT.Copy).then_inc(S["x1t"], 1)
                    act.wait_ge(S["tc1"], e + 1)
                    a.activation(r["la"], r["tc"], ACT.Ln, bias=1.0, scale=1.0)
                    a.activation(r["lb"], r["tc"], ACT.Ln, bias=1.0, scale=-1.0).then_inc(S["ln1"], 1)
                if q == K_SQ1:
                    act.wait_ge(S["mx"], e + 1)
                    for t in range(BLK):
                        a.activation(JUNK[:, blk(t)], E[:, t, 0:P], ACT.Square, accum_out=small["m2"][:, t:t + 1])
                    a.activation(r["pxy"], E[:, :, P], ACT.Copy).then_inc(S["sq1"], 1)
                if q == K_TQ:
                    act.wait_ge(S["q"], e + 1)
                    a.activation(r["tq"], r["q"], ACT.Tanh).then_inc(S["tq"], 1)
                if q == K_H:
                    act.wait_ge(S["alphabeta"], e + 1)
                    for t in range(BLK):
                        a.activation(HY[:, blk(t)], E[:, t, 0:P], ACT.Copy, scale=small["alpha"][:, t:t + 1]).then_inc(S["scaled"], 1)
                if q == K_LN2:
                    act.wait_ge(S["h"], e + 1)
                    for t in range(BLK):
                        last = a.activation(JUNK[:, blk(t)], HY[:, blk(t)], ACT.Square, accum_out=small["h2"][:, t:t + 1])
                    last.then_inc(S["sq2"], 1)
                    act.wait_ge(S["tc2"], e + 1)
                    a.activation(r["la"], r["tc"], ACT.Ln, bias=1.0, scale=1.0)
                    a.activation(r["lb"], r["tc"], ACT.Ln, bias=1.0, scale=-1.0).then_inc(S["ln2"], 1)
                if q == K_XT:
                    act.wait_ge(S["kap"], e + 1)
                    for t in range(BLK):
                        a.activation(XTH[:, bass.ds(e * CW + t * P, P)], HY[:, blk(t)], ACT.Copy,
                                     scale=small["kap"][:, t:t + 1]).then_inc(S["xth"], 1)

            def result(k, e, G):
                if k == slot_of(3, G):
                    act.wait_ge(S["s2_tr"], e + 1)
                    a.activation(TH[:, :], E[:, 0, :], ACT.Relu).then_inc(S["act_link"], 1)
                    for t in range(BLK):
                        a.activation(JUNK[:, blk(t)], E[:, 0, blk(t)], ACT.Square, accum_out=small["s2"][:, t:t + 1])
                    act.wait_ge(S["act_link"], e + 1)
                    for t in range(BLK):
                        last = a.activation(X1T[:, blk(t)], TH[:, blk(t)], ACT.Square, accum_out=small["r2"][:, t:t + 1])
                    last.then_inc(S["sq3"], 1)
                if k == slot_of(5, G):
                    act.wait_ge(S["n3"], e + 1)
                    a.activation(r["tq"], r["t"], ACT.Tanh).then_inc(S["th3"], 1)

            def body(phase, c, lw, n0):
                q0 = lw if phase == 2 else 0
                for q in range(q0, NCH):
                    split_high(q, n0, q0)
                    if phase == 1 and not isinstance(c, int):
                        chunk_end(q, c - 1)
                    elif phase == 2 and isinstance(c, int):
                        chunk_end(q, NCH - 1)
                    elif phase == 2:
                        result(q - q0, c - 1, NCH - q0)
            steps(act, body)
            for k in range(NCH):
                result(k, NCH - 1, NCH)

        @block.vector
        def _(dve):
            v = nc.vector
            r = {k: t[:, :] for k, t in small.items()}
            link = Link(dve, S["dve_link"])
            dve.wait_ge(S["urow"], 16)
            v.tensor_scalar(U[:, :], U[:, :], U_EPS, 1.0, ALU.max, ALU.min).then_inc(S["gum1"], 1)
            dve.wait_ge(S["gum2"], 1)
            v.tensor_scalar(U[:, :], U[:, :], -1.0, U_EPS, ALU.mult, ALU.add).then_inc(S["gum1"], 1)
            dve.wait_ge(S["weights"], 16 * 7)
            v.tensor_scalar(RX[:, P:2 * P], RX[:, P:2 * P], 0.5, None, ALU.mult)
            v.tensor_scalar(RS[:, P:2 * P], RS[:, P:2 * P], -0.5, None, ALU.mult).then_inc(S["wt_scaled"], 1)
            dve.wait_ge(S["vecs"], 160)
            dve.wait_ge(S["const"], 1)
            link(v.tensor_tensor(B3[:, P:2 * P], B3[:, P:2 * P], B3[:, 2 * P:3 * P], ALU.subtract))
            link(v.tensor_scalar(B3[:, P:2 * P], B3[:, P:2 * P], 0.5, None, ALU.mult))
            for row in (0, 32):
                v.tensor_copy(BP[row:row + 1, :], B3[row:row + 1, :])
                link(v.tensor_copy(BR[:, :], B3[:, :]))
                link(v.tensor_tensor(B3[:, :], B3[:, :], BR[:, :], ALU.subtract))
            v.tensor_copy(BP[64:65, :], B3[64:65, :]).then_inc(S["bias_ready"], 1)
            if first_low < NCH:
                v.memset(PART[:, 0, :], 0.0)

            def stats(src, mv, done):
                for t in range(BLK):
                    last = v.bn_stats(BS[:, t, :], src[:, blk(t)])
                link(last)
                dve.nop(nofuse=True)
                for t in range(BLK):
                    last = v.bn_aggr(mv[:, t, :], BS[:, t, :])
                last.then_inc(S[done], 1)

            SETUP = link.n
            def prelude(h):
                nonlocal link
                link = Link(dve, S["dve_link"], SETUP + 2 * h)
                for k, buf in enumerate((XR, FU)):
                    dve.wait_ge(S[f"xin{k}"], 16 * (h + 1))
                    stats(buf, MV, "pre_stats")
                    dve.wait_ge(S["pre_rs"], 2 * h + k + 1)
                    wait_n(dve, "pre_xn", 2 * h + k)
                    for t in range(BLK):
                        last = v.tensor_scalar(TH[:, blk(t)], buf[:, blk(t)], MV[:, t, 0:1],
                                               small["rs"][:, t:t + 1], ALU.subtract, ALU.mult)
                    last.then_inc(S["pre_z"], 1)
            prelude(0)
            with dve.Fori(1, NCH // 2) as h:
                prelude(h)
            assert link.n == 2
            link = Link(dve, S["dve_link"], SETUP + NCH)
            dve.wait_ge(S["gum2"], 2)
            dve.wait_ge(S["pre_logit"], NCH)
            link(v.scalar_tensor_tensor(out=LG[:, :, :].rearrange("p b k -> p (b k)"), in0=U[:, :], scalar=-1.0,
                                        in1=E[:, 1, 0:2 * NB], op0=ALU.mult, op1=ALU.add))
            link(v.tensor_tensor(LG[:, :, :], LG[:, :, :],
                                 BNB[:, :].rearrange("p (o k) -> p o k", o=1).to_broadcast([P, NB, 2]), ALU.add))
            link(v.tensor_tensor(TOP[:, :], LG[:, :, 0], LG[:, :, 1], ALU.max))
            v.tensor_tensor(LG[:, :, 0], LG[:, :, 0], TOP[:, :], ALU.subtract)
            v.tensor_tensor(LG[:, :, 1], LG[:, :, 1], TOP[:, :], ALU.subtract).then_inc(S["gate_arg"], 1)
            dve.wait_ge(S["gate_exp"], 1)
            link(v.tensor_tensor(SM[:, :], LG[:, :, 0], LG[:, :, 1], ALU.add))
            link(v.reciprocal(SM[:, :], SM[:, :]))
            v.tensor_tensor(LG[:, :, 0], LG[:, :, 0], SM[:, :], ALU.mult)
            link(v.tensor_tensor(LG[:, :, 1], LG[:, :, 1], SM[:, :], ALU.mult))
            link(v.tensor_tensor(TOP[:, :], LG[:, :, 1], LG[:, :, 0], ALU.is_gt))
            link(v.tensor_tensor(TOP[:, :], TOP[:, :], LG[:, :, 1], ALU.add))
            v.tensor_tensor(GATE[:, :], TOP[:, :], LG[:, :, 1], ALU.subtract).then_inc(S["gates"], 1)
            dve.wait_ge(S["gates"], 1)
            DONE = SETUP + NCH + link.n
            dve.wait_ge(S["xn_kept"], NCH)
            with dve.Fori(0, NCH) as q:
                rows = v4(XN[:, bass.ds(q * CW, CW)])
                v.tensor_tensor(rows, rows, GATE[:, bass.ds(q * BLK, BLK)].rearrange("p (b o) -> p b o", o=1)
                                .to_broadcast([P, BLK, P]), ALU.mult).then_inc(S["gated"], 1)
            with dve.Fori(0, NCH) as q:
                cols = bass.ds(q * CW, CW)
                dve.wait_ge(S["xgh"], q + 1)
                v.tensor_tensor(XGL[:, cols], XN[:, cols], XGH[:, cols].bitcast(F32), ALU.subtract).then_inc(S["xgl"], 1)

            def split_low(q, n0, q0):
                n = n0 + (q - q0)
                dve.wait_ge(S["hi"], n + 1)
                v.tensor_tensor(AL[:, q % 2, :], A[:, q % RING, :], AH[:, q % 2, :].bitcast(F32),
                                ALU.subtract).then_inc(S["lo"], 1)

            K1 = 6

            def chunk_end(q, e, n_end):
                if q == K_GATED:
                    dve.wait_ge(S["used"], n_end)
                    dve.wait_ge(S["epi_in"], 48 * (e + 1))
                    v.tensor_tensor(GB[:, :], ACC[:, bass.ds((e % 2) * CW, CW)], GB[:, :],
                                    ALU.mult).then_inc(S["s1_gated"], 1)
                if q == K_TANH:
                    dve.wait_ge(S["tanh"], e + 1)
                    link(v.scalar_tensor_tensor(out=v4(FU[:, :]), in0=v4(TH[:, :]), scalar=1.0,
                                                in1=E[:, :, P:2 * P], op0=ALU.add, op1=ALU.mult))
                    link(v.tensor_tensor(v4(FU[:, :]), v4(FU[:, :]), E[:, :, 2 * P:3 * P], ALU.add))
                    link(v.tensor_tensor(FU[:, :], FU[:, :], XR[:, :], ALU.add))
                    stats(FU, MV, "stats1")
                if q == K_PRE:
                    dve.wait_ge(S["rs1"], e + 1)
                    for t in range(BLK):
                        last = v.scalar_tensor_tensor(out=FU[:, blk(t)], in0=FU[:, blk(t)], scalar=MV[:, t, 0:1],
                                                      in1=GOUT[:, :], op0=ALU.subtract, op1=ALU.mult)
                    last.then_inc(S["centered"], 1)
                    dve.wait_ge(S["centered"], e + 1)
                    dve.wait_ge(S["xb"], e + 1)
                    for t in range(BLK):
                        last = v.scalar_tensor_tensor(out=FU[:, blk(t)], in0=FU[:, blk(t)],
                                                      scalar=small["rs"][:, t:t + 1], in1=XR[:, blk(t)],
                                                      op0=ALU.mult, op1=ALU.add)
                    link(last)
                    stats(FU, MV2, "stats2")
                if q == K_X1:
                    dve.wait_ge(S["rs2"], e + 1)
                    for t in range(BLK):
                        last = v.tensor_scalar(X1[:, blk(t)], FU[:, blk(t)], MV2[:, t, 0:1],
                                               small["rs2"][:, t:t + 1], ALU.subtract, ALU.mult)
                    last.then_inc(S["x1_ready"], 1)
                if q == K_H:
                    for t in range(BLK):
                        dve.wait_ge(S["scaled"], BLK * e + t + 1)
                        last = v.scalar_tensor_tensor(out=HY[:, blk(t)], in0=HB[:, :],
                                                      scalar=small["beta"][:, t:t + 1], in1=HY[:, blk(t)],
                                                      op0=ALU.mult, op1=ALU.add)
                    last.then_inc(S["h"], 1)
                if q == K_XT:
                    for t in range(BLK):
                        cols = bass.ds(e * CW + t * P, P)
                        dve.wait_ge(S["xth"], BLK * e + t + 1)
                        last = v.scalar_tensor_tensor(out=XTL[:, cols], in0=HY[:, blk(t)],
                                                      scalar=small["kap"][:, t:t + 1], in1=XTH[:, cols].bitcast(F32),
                                                      op0=ALU.mult, op1=ALU.subtract)
                    last.then_inc(S["xtl"], 1)

            K3 = 2

            def result(k, e, G, n_end, with_part):
                if k == slot_of(1, G):
                    dve.wait_ge(S["used"], n_end)
                    dve.wait_ge(S["l0_mm"], NCH)
                    acc = ACC[:, bass.ds((e % 2) * CW + 2 * CW, CW)]
                    if with_part:
                        v.tensor_tensor(GB[:, :], acc, PART[:, e - (first_low - 1), :], ALU.add).then_inc(S["s2_taken"], 1)
                    else:
                        v.tensor_copy(GB[:, :], acc).then_inc(S["s2_taken"], 1)
                if k == slot_of(8, G):
                    dve.wait_ge(S["coef"], 2 * e + 2)
                    dve.wait_ge(S["x1_back"], 16 * (e + 1))
                    for t in range(BLK):
                        last = v.scalar_tensor_tensor(out=FU[:, blk(t)], in0=TH[:, blk(t)],
                                                      scalar=small["kap"][:, t:t + 1], in1=XR[:, blk(t)],
                                                      op0=ALU.mult, op1=ALU.add)
                    link(last)
                    stats(FU, MV, "stats3")
                if k == slot_of(9, G):
                    dve.wait_ge(S["rs3"], 2 * e + 2)
                    dve.wait_ge(S["x1_stored"], 16 * NCH)
                    for t in range(BLK):
                        last = v.tensor_scalar(X1[:, blk(t)], FU[:, blk(t)], MV[:, t, 0:1],
                                               small["rs"][:, t:t + 1], ALU.subtract, ALU.mult)
                    last.then_inc(S["res"], 1)

            def body(phase, c, lw, n0):
                nonlocal link
                q0 = lw if phase == 2 else 0
                if phase == 1 and not isinstance(c, int):
                    link = Link(dve, S["dve_link"], DONE + K1 * (c - 1))
                elif phase == 2 and isinstance(c, int):
                    link = Link(dve, S["dve_link"], DONE + K1 * (NCH - 1))
                elif phase == 2:
                    link = Link(dve, S["dve_link"], DONE + K1 * NCH + K3 * (c - 1))
                for q in range(q0, NCH):
                    split_low(q, n0, q0)
                    if phase == 1 and lw and q == min(lw + 2, NCH - 1):
                        dve.wait_ge(S["used"], n0 + lw)
                        v.tensor_copy(PART[:, c - (first_low - 1), :],
                                      ACC[:, bass.ds((c % 2) * CW + 2 * CW, CW)]).then_inc(S["part_saved"], 1)
                    if phase == 1 and not isinstance(c, int):
                        chunk_end(q, c - 1, n0)
                    elif phase == 2 and isinstance(c, int):
                        chunk_end(q, NCH - 1, n0)
                    elif phase == 2:
                        result(q - q0, c - 1, NCH - q0, n0, lw > 0)
                if phase == 2 and not isinstance(c, int):
                    assert link.n == K3, link.n
                elif phase == 2 or not isinstance(c, int):
                    assert link.n == K1, link.n
            steps(dve, body)
            link = Link(dve, S["dve_link"], DONE + K1 * NCH + K3 * (NCH - 1))
            for k in range(NCH):
                result(k, NCH - 1, NCH, TOTAL, first_low < NCH)

        @block.tensor
        def _(pe):
            p = nc.tensor
            pe.wait_ge(S["weights"], 16 * 7)
            pe.wait_ge(S["ident_ready"], 2)
            pe.wait_ge(S["hb_ready"], 1)
            p.transpose(E[:, 3, 0:P], WH[:, :], ident[:, :])
            p.matmul(E[:, 3, P:P + 1], WH[:, :], HBC[:, :], start=True, stop=True).then_inc(S["rm_psum"], 1)
            def prelude(h):
                for k, xt in enumerate((XNT, X1T)):
                    q = 2 * h + k
                    pe.wait_ge(S["pre_xn"], q + 1)
                    wait_n(pe, "pre_xt", q)
                    for t in range(BLK):
                        last = p.transpose(E[:, 0, blk(t)], PART[:, 1 + k, blk(t)], ident[:, :])
                    last.then_inc(S["pre_tr"], 1)
                    pe.wait_ge(S["pre_xt"], q + 1)
                    for t in range(BLK):
                        last = p.matmul(E[:, 1, bass.ds(q * 2 * BLK + 2 * t, 2)], xt[:, blk(t)], WN[:, :],
                                        start=True, stop=True)
                    last.then_inc(S["pre_logit"], 1)
            prelude(0)
            with pe.Fori(1, NCH // 2) as h:
                prelude(h)
            pe.wait_ge(S["gates"], 1)
            p.transpose(E[0:NB, 2, 0:P], GATE[:, :], ident[:, :]).then_inc(S["gate_tr"], 1)

            def chunk_end(q, e):
                if q == K_GATED:
                    pe.wait_ge(S["s1_gated"], e + 1)
                    pe.wait_ge(S["epi_in"], 48 * (e + 1))
                    for t in range(BLK):
                        p.matmul(E[:, t, 0:3 * P], ones[:, :], BP[:, :], start=True, stop=False)
                        p.matmul(E[:, t, 0:2 * P], XNT[:, blk(t)], RX[:, :], start=False, stop=False)
                        last = p.matmul(E[:, t, 0:3 * P], GB[:, blk(t)], RS[:, :], start=False, stop=True)
                    last.then_inc(S["l0_mm"], 1)
                if q == K_X1:
                    pe.wait_ge(S["x1_ready"], e + 1)
                    for t in range(BLK):
                        last = p.transpose(E[:, 0, blk(t)], X1[:, blk(t)], ident[:, :])
                    last.then_inc(S["x1_tr"], 1)
                if q == K_X1T:
                    pe.wait_ge(S["x1t"], e + 1)
                    for t in range(BLK):
                        last = p.matmul(E[:, t, 0:P + 1], X1T[:, blk(t)], RM[:, :], start=True, stop=True)
                    last.then_inc(S["mx"], 1)

            def three_pass(acc, hi, lo, q, t, start, stop):
                st = blk(BLK * q + t)
                mv = slice(t * CW, (t + 1) * CW)
                p.matmul(acc, hi[:, st], AH[:, q % 2, mv], start=start, stop=False)
                p.matmul(acc, hi[:, st], AL[:, q % 2, mv], start=False, stop=False)
                return p.matmul(acc, lo[:, st], AH[:, q % 2, mv], start=False, stop=stop)

            def body(phase, c, lw, n0):
                q0 = lw if phase == 2 else 0
                acc1 = ACC[:, bass.ds((c % 2) * CW, CW)]
                acc2 = ACC[:, bass.ds((c % 2) * CW + 2 * CW, CW)]
                if phase == 1:
                    if lw:
                        pe.wait_ge(S["xtl"], c - 1)
                elif isinstance(c, int):
                    pe.wait_ge(S["s1_gated"], NCH - 1)
                else:
                    pe.wait_ge(S["s1_gated"], NCH)
                for q in range(q0, NCH):
                    if phase == 1 and isinstance(c, int):
                        pe.wait_ge(S["xgl"], q + 1)
                    if phase == 2 and isinstance(c, int):
                        pe.wait_ge(S["xtl"], q + 1)
                    pe.wait_ge(S["lo"], n0 + (q - q0) + 1)
                    for t in range(BLK):
                        if phase == 1:
                            last = three_pass(acc1, XGH, XGL, q, t, q == 0 and t == 0, q == NCH - 1 and t == BLK - 1)
                            if q < lw:
                                last = three_pass(acc2, XTH, XTL, q, t, q == 0 and t == 0, q == lw - 1 and t == BLK - 1)
                        else:
                            last = three_pass(acc2, XTH, XTL, q, t, q == q0 and t == 0, q == NCH - 1 and t == BLK - 1)
                    last.then_inc(S["used"], 1)
                    if phase == 1 and not isinstance(c, int):
                        chunk_end(q, c - 1)
                    elif phase == 2 and isinstance(c, int):
                        chunk_end(q, NCH - 1)
                    elif phase == 2:
                        result(q - q0, c - 1, NCH - q0)

            def result(k, e, G):
                if k == slot_of(1, G):
                    pe.wait_ge(S["s2_taken"], e + 1)
                    pe.wait_ge(S["scaled"], BLK * NCH)
                    for t in range(BLK):
                        last = p.transpose(E[:, 0, blk(t)], GB[:, blk(t)], ident[:, :])
                    last.then_inc(S["s2_tr"], 1)
            pe.wait_ge(S["rm_ready"], 1)
            pe.wait_ge(S["wt_scaled"], 1)
            pe.wait_ge(S["bias_ready"], 1)
            steps(pe, body)
            for k in range(NCH):
                result(k, NCH - 1, NCH)


_INS = ["x", "adjT", "u", "w1", "b1", "w2", "b2", "wg", "bg", "wn", "bn", "g_in", "b_in", "g_out", "b_out",
        "w_hyp", "b_hyp"]


def kernel(**inputs):
    import numpy as np
    import concourse.bacc as bacc
    from concourse.bass_utils import run_bass_kernel_spmd as run

    given = {k: np.asarray(v) for k, v in inputs.items()}
    n, d = given["x"].shape
    nch = n // CW
    host = {
        "x": given["x"].reshape(nch, BLK, P, d).transpose(0, 2, 1, 3).reshape(nch * P, CW),
        "adjT": given["adj"].reshape(nch, CW, nch, BLK, P).transpose(0, 2, 4, 3, 1).reshape(nch * nch * P, GW),
        "u": given["L0_gnn_u"].reshape(n // P, P, 2).transpose(1, 0, 2).reshape(P, n // P * 2),
        "w1": given["L0_gnn_W1"], "b1": given["L0_gnn_b1"], "w2": given["L0_gnn_W2"], "b2": given["L0_gnn_b2"],
        "wg": given["L0_gnn_Wg"], "bg": given["L0_gnn_bg"], "wn": given["L0_gnn_Wn"], "bn": given["L0_gnn_bn"],
        "g_in": given["L0_gnn_g_in"], "b_in": given["L0_gnn_b_in"], "g_out": given["L0_gnn_g_out"],
        "b_out": given["L0_gnn_b_out"], "w_hyp": given["L1_gnn_weight"], "b_hyp": given["L1_gnn_bias"],
    }
    nc = bacc.Bacc("TRN2", target_bir_lowering=False, num_devices=1)
    arrays, args = {}, []
    for name in _INS:
        a = np.ascontiguousarray(host[name])
        arrays[f"in_{name}_dram"] = a
        args.append(nc.dram_tensor(f"in_{name}_dram", a.shape, mybir.dt.from_np(a.dtype), kind="ExternalInput").ap())
    args.append(nc.dram_tensor("out_0_dram", (nch * P, CW), F32, kind="ExternalOutput").ap())
    build(nc, *args)
    r = run(nc, [arrays], core_ids=[0])
    got = r.results[0]["out_0_dram"]
    return got.reshape(nch, P, BLK, d).transpose(0, 2, 1, 3).reshape(n, d)
```

```python
from contextlib import ExitStack

import concourse.bass as bass
from concourse import mybir

F32 = mybir.dt.float32
F32R = mybir.dt.float32r
BF16 = mybir.dt.bfloat16
ALU = mybir.AluOpType
ACT = mybir.ActivationFunctionType

P = 128
BLK = 4
CW = BLK * P
GW = BLK * CW
RING = 4
HW = GW // 2
SPLITS = 4
LN_EPS = 1e-5
U_EPS = 1e-10
MIN_NORM = 1e-15
MIN_NORM2 = 1e-30
MAX_NORM = 0.996
ATANH_CLIP = 0.9999998807907104
ATANH_MAX_NORM = 3.1063027
SERIES_BELOW2 = 0.0025


def low(c):
    return RING * ((c - 2) // RING) if c >= 2 else 0


def bands(first, nch):
    out = []
    for c in range(first, nch):
        if out and out[-1][2] == low(c):
            out[-1][1] = c + 1
        else:
            out.append([c, c + 1, low(c)])
    return [tuple(b) for b in out]


def build(nc, x, adjT, u, w1, b1, w2, b2, wg, bg, wn, bn, g_in, b_in, g_out, b_out, w_hyp, b_hyp, out):
    N = x.shape[0] * x.shape[1] // P
    NCH = N // CW
    NB = N // P
    N1 = NCH * NCH
    assert NCH % RING == 0

    with ExitStack() as ctx:
        def sb(name, shape, dt=F32):
            return ctx.enter_context(nc.sbuf_tensor(name, shape, dt))

        def sem(name):
            return ctx.enter_context(nc.semaphore(name))

        A = sb("A", [P, RING, GW])
        AH = sb("AH", [P, SPLITS, HW], F32R)
        AL = sb("AL", [P, SPLITS, HW], F32R)
        XGH = sb("XGH", [P, N], F32R)
        XGL = sb("XGL", [P, N], F32R)
        XTH = sb("XTH", [P, N], F32R)
        XTL = sb("XTL", [P, N], F32R)
        first_low = min([c for c in range(NCH) if low(c)] or [NCH])
        PART = sb("PART", [P, NCH - first_low + 1, CW])
        XR = sb("XR", [P, CW])
        XNT = sb("XNT", [P, CW])
        GB = sb("GB", [P, CW])
        TH = sb("TH", [P, CW])
        FU = sb("FU", [P, CW])
        X1 = sb("X1", [P, CW])
        X1T = sb("X1T", [P, CW])
        HY = sb("HY", [P, CW])
        JUNK = sb("JUNK", [P, CW])
        ident = sb("ident", [P, P])
        RX = sb("RX", [P, 2 * P])
        RS = sb("RS", [P, 3 * P])
        RM = sb("RM", [P, P + 1])
        WH = sb("WH", [P, P])
        WN = sb("WN", [P, 2])
        GIN = sb("GIN", [P, P])
        BIN = sb("BIN", [P, P])
        GOUT = sb("GOUT", [P, P])
        BOUT = sb("BOUT", [P, P])
        HB = sb("HB", [P, P])
        HBC = sb("HBC", [P, 1])
        BNB = sb("BNB", [P, 2])
        B3 = sb("B3", [P, 3 * P])
        BP = sb("BP", [P, 3 * P], BF16)
        BR = sb("BR", [P, 3 * P], BF16)
        ones = sb("ones", [P, P], BF16)
        NHALF = sb("NHALF", [P, NB])
        NEG1 = sb("NEG1", [P, BLK])
        U = sb("U", [P, NB * 2])
        LG = sb("LG", [P, NB, 2])
        TOP = sb("TOP", [P, NB])
        SM = sb("SM", [P, NB])
        GATE = sb("GATE", [P, NB])
        GATET = sb("GATET", [NB, P])
        BS = sb("BS", [P, BLK, 6])
        MV = sb("MV", [P, BLK, 2])
        MV2 = sb("MV2", [P, BLK, 2])
        small = {n: sb("r_" + n, [P, BLK]) for n in (
            "v", "rs", "rs2", "n2", "t", "fx", "m2", "pxy", "minv", "q", "sq", "cf", "coef",
            "n2_1", "inv_1", "t_1", "tc_1", "la_1", "lb_1", "ser_1", "mask_1",
            "n2_2", "inv_2", "t_2", "tc_2", "la_2", "lb_2", "ser_2", "mask_2",
            "tq", "rsc", "x2", "xy", "a", "b", "den", "alpha", "beta", "h2", "kap", "s2", "r2", "w", "nr", "thn")}
        y2 = sb("y2", [P, 1])
        hbs = sb("hbs", [P, 5])

        ACC = ctx.enter_context(nc.psum_tensor("ACC", [P, 4 * CW], F32))
        E = ctx.enter_context(nc.psum_tensor("E", [P, 4, CW], F32))

        xnt_dram = nc.dram_tensor("xnt_scratch", [NCH * P, CW], F32).ap()
        gate_dram = nc.dram_tensor("gate_scratch", [NCH, CW], F32).ap()
        x1_dram = nc.dram_tensor("x1_scratch", [NCH * P, CW], F32).ap()

        S = {}
        for name in (
                "act_link", "front_link", "rstd_link", "gate_link", "gate_hard", "pre_scaled", "xin2", "back_link", "result_link", "stats_link", "alphabeta", "bias_ready", "centered", "coef", "const", "dve_link",
                "epi_in", "gate_arg", "gate_exp", "gate_rows", "gate_stored", "gate_tr", "gated",
                "gates", "gum1", "gum2", "h", "hb_norm", "hb_ready", "hb_sq", "hb_tanh", "hi",
                "ident_ready", "kap", "l0_mm", "ld0", "ld1", "ld2", "ld3", "ln1", "ln2", "lo", "mx",
                "n3", "part_saved", "pool_link", "pre_logit", "pre_rs", "pre_stats", "pre_tr",
                "pre_xn", "pre_xt", "pre_z", "q", "res", "res_stored", "rm_psum", "rm_ready", "rs1",
                "rs2", "rs3", "s1_gated", "s2_taken", "s2_tr", "scaled", "sq1", "sq2", "sq3",
                "stats1", "stats2", "stats3", "tanh", "tc1", "tc2", "th3", "tq", "urow", "used",
                "vecs", "weights", "wt_scaled", "x1_back", "x1_ready", "x1_stored", "x1_tr", "x1t",
                "xb", "xgh", "xgl", "xin0", "xin1", "xnt_stored0", "xn_kept", "xnt_stored1", "xth", "xtl",
                "y2_ready"):
            S[name] = sem("s_" + name)

        block = ctx.enter_context(nc.Block())

        class Link:

            def __init__(self, eng, s, base=0, nop=False):
                self.eng, self.s, self.base, self.nop, self.n = eng, s, base, nop, 0

            def __call__(self, ins):
                self.n += 1
                ins.then_inc(self.s, 1)
                self.eng.wait_ge(self.s, self.base + self.n)
                if self.nop:
                    self.eng.nop(nofuse=True)

        def wait_n(eng, name, value):
            if not (isinstance(value, int) and value <= 0):
                eng.wait_ge(S[name], value)

        def b4(ap):
            return ap.rearrange("p (o d) -> p o d", o=1).to_broadcast([P, BLK, P])

        def v4(ap):
            return ap.rearrange("p (b d) -> p b d", b=BLK)

        def blk(t):
            return slice(t * P, (t + 1) * P)

        PB = 3
        assert NCH % (2 * PB) == 0 and NCH - first_low >= 2 * PB

        def prelude(eng, main, gates=None):
            def pair(h):
                for side in range(2):
                    main(2 * PB * h + PB * side, side, 2 * h + side)
                    b = 2 * h + side - 1
                    if gates and not (isinstance(b, int) and b < 0):
                        gates(b, 1 - side)
            pair(0)
            with eng.Fori(1, NCH // (2 * PB)) as h:
                pair(h)
            if gates:
                gates(NCH // PB - 1, 1)

        def norm_rows(side, i):
            return PART[:, 1 + PB * side + i, :]

        def par(side, i):
            return (PB * side + i) % 2

        LAST = NCH - 2
        order = ([(0, q) for q in range(LAST)] + [(1, q) for q in range(LAST)] + [(2, q) for q in range(LAST - RING - 2)]
                 + [(0, LAST), (0, LAST + 1), (1, LAST), (1, LAST + 1)]
                 + [(2, q) for q in range(LAST - RING - 2, NCH)])
        assert low(2) == 0 and len(order) == 3 * NCH
        FRONT = 3
        START2 = N1 + FRONT * NCH

        def phase2_base():
            base, n = {}, START2
            for lo_c, hi_c, lw in bands(FRONT, NCH):
                base[lo_c] = n
                n += (hi_c - lo_c) * (NCH - lw)
            return base, n
        BASE2, TOTAL = phase2_base()

        class Step:
            def __init__(self, phase, c, groups, n0, lw=0, front=None, back=None, result1=None, result2=None):
                self.phase, self.c, self.groups, self.n0, self.lw = phase, c, groups, n0, lw
                self.front, self.back = front, back
                self.result1, self.result2 = result1, result2
                self.places = result_places(len(groups))
                self.mixed = phase == 2 and isinstance(c, int)

            def halves(self):
                for k, (d, q) in enumerate(self.groups):
                    for h in range(2):
                        yield 2 * k + h, k, h, d, q

        def steps(eng, body):
            whole = [(0, q) for q in range(NCH)]
            body(Step(1, 0, whole, 0))
            body(Step(1, 1, whole, NCH, front=0))
            for c0, c1, lw in bands(2, NCH):
                with eng.Fori(c0, c1) as c:
                    body(Step(1, c, whole, NCH * c, lw, front=c - 1, back=c - 2))
            body(Step(2, 0, order[0:NCH], N1, front=NCH - 1, back=NCH - 2))
            body(Step(2, 0, order[NCH:2 * NCH], N1 + NCH, back=NCH - 1))
            body(Step(2, 0, order[2 * NCH:], N1 + 2 * NCH))
            for c0, c1, lw in bands(FRONT, NCH):
                with eng.Fori(c0, c1) as c:
                    body(Step(2, c, [(0, q) for q in range(lw, NCH)], BASE2[c0] + (NCH - lw) * (c - c0), lw,
                              result1=c - 1, result2=c - 2))

        def at(k):
            return k * NCH // 12
        GATED, L0, TANH, FUSE, STATS1, CENTER, STATS2, X1_AT, X1_TR, X1T_AT, MX = (
            at(k) for k in (2, 2, 9, 10, 11, 14, 15, 17, 17, 21, 22))
        MX_OUT, TQ, SCALE, H_AT, SQ2, LN, XT = (at(k) for k in (2, 5, 10, 11, 13, 19, 21))

        def result_places(groups):
            last = 2 * groups - 1
            return {"add": 0, "take": 1, "turn": 1, "relu": 5, "norm": 5, "tanh": min(9, last)}

        third = {("take", 0): 5, ("turn", 0): 5, ("relu", 0): 9, ("tanh", 0): 13,
                 ("add", 0): 16, ("take", 1): 17, ("turn", 1): 17, ("relu", 1): 21, ("norm", 0): 20, ("tanh", 1): 23}
        third_used = {0: 2, 1: 4}

        def results(step, j):
            if step.mixed:
                if isinstance(step.n0, int) and step.n0 == N1 + 2 * NCH:
                    return [(ev, e, 2 * (step.n0 + third_used[e])) for (ev, e), place in third.items() if place == j]
                return []
            if step.phase == 1:
                return []
            return [(ev, step.result2 if ev in ("add", "norm") else step.result1, 2 * step.n0)
                    for ev, place in step.places.items() if place == j]

        def tail():
            return [("add", NCH - 2), ("take", NCH - 1), ("turn", NCH - 1), ("relu", NCH - 1), ("norm", NCH - 2),
                    ("tanh", NCH - 1), ("add", NCH - 1), ("norm", NCH - 1)]

        @block.sync
        def _(sp):
            sp.dma_start(RX[:, 0:P], wg[0:P, :]).then_inc(S["weights"], 16)
            sp.dma_start(RX[:, P:2 * P], w1).then_inc(S["weights"], 16)
            sp.dma_start(RS[:, 0:P], wg[P:2 * P, :]).then_inc(S["weights"], 16)
            sp.dma_start(RS[:, P:2 * P], w2).then_inc(S["weights"], 16)
            sp.dma_start(RS[:, 2 * P:3 * P], w2).then_inc(S["weights"], 16)
            sp.dma_start(WH[:, :], w_hyp).then_inc(S["weights"], 16)
            sp.dma_start(WN[:, :], wn).then_inc(S["weights"], 16)
            for t, v in ((GIN[:, :], g_in), (BIN[:, :], b_in), (GOUT[:, :], g_out), (BOUT[:, :], b_out),
                         (HB[:, :], b_hyp), (B3[:, 0:P], bg), (B3[:, P:2 * P], b1), (B3[:, 2 * P:3 * P], b2),
                         (BNB[:, :], bn)):
                sp.dma_start(t, v.partition_broadcast(P)).then_inc(S["vecs"], 16)
            sp.dma_start(HBC[:, :], b_hyp.rearrange("(p o) -> p o", o=1)).then_inc(S["vecs"], 16)
            sp.dma_start(U[:, :], u).then_inc(S["urow"], 16)

            XIN = (XR, FU, GB)

            def load_x(q, i):
                sp.dma_start(XIN[i][:, :], x[bass.ds(q * P, P), :]).then_inc(S[f"xin{i}"], 16)

            def store_xnt(q, k):
                sp.wait_ge(S["pre_xt"], q + 1)
                sp.dma_start(xnt_dram[bass.ds(q * P, P), :], (XNT, X1T)[k][:, :]).then_inc(S[f"xnt_stored{k}"], 16)
            for i in range(PB):
                load_x(i, i)
            for q in range(RING):
                sp.dma_start(A[:, q, :], adjT[bass.ds(q * P, P), :]).then_inc(S[f"ld{q}"], 16)

            def sp_prelude(h, last):
                for side in range(2):
                    for i in range(PB):
                        q = 2 * PB * h + PB * side + i
                        if not (last and side):
                            sp.wait_ge(S["pre_z"], q + 1)
                            load_x(q + PB, i)
                        store_xnt(q, par(side, i))
            with sp.Fori(0, NCH // (2 * PB) - 1) as h:
                sp_prelude(h, False)
            sp_prelude(NCH // (2 * PB) - 1, True)
            sp.wait_ge(S["gate_rows"], 1)
            sp.dma_start(gate_dram.rearrange("c (t p) -> (c t) p", p=P), GATET[:, :]).then_inc(S["gate_stored"], 16)

            def body(step):
                for k, (d, q) in enumerate(step.groups):
                    n = step.n0 + k
                    if step.phase == 1 and k == NCH - 2:
                        c = step.c
                        if isinstance(c, int) and c == 0:
                            sp.wait_ge(S["gate_stored"], 16)
                            sp.wait_ge(S["xnt_stored0"], 16 * (NCH // 2))
                            sp.wait_ge(S["xnt_stored1"], 16 * (NCH // 2))
                        wait_n(sp, "stats2", c)
                        wait_n(sp, "l0_mm", c)
                        sp.dma_start(XR[:, :], x[bass.ds(c * P, P), :]).then_inc(S["epi_in"], 16)
                        sp.dma_start(XNT[:, :], xnt_dram[bass.ds(c * P, P), :]).then_inc(S["epi_in"], 16)
                        sp.dma_start(GB[:, :], gate_dram[bass.ds(c, 1), :].partition_broadcast(P)
                                     ).then_inc(S["epi_in"], 16)
                    if isinstance(n, int) and n < RING:
                        continue
                    sp.wait_ge(S["lo"], 2 * (n - RING + 1))
                    sp.dma_start(A[:, k % RING, :],
                                 adjT[bass.ds(((step.c + d) * NCH + q) * P, P), :]).then_inc(S[f"ld{k % RING}"], 16)
            steps(sp, body)

        @block.gpsimd
        def _(pool):
            g = nc.gpsimd
            r = {k: v[:, :] for k, v in small.items()}
            g.memset(ident[:, :], 0.0).then_inc(S["ident_ready"], 1)
            g.memset(ones[:, :], 1.0)
            g.memset(NHALF[:, :], -0.5)
            g.memset(NEG1[:, :], -1.0)
            g.memset(BP[:, :], 0.0).then_inc(S["const"], 1)
            pool.wait_ge(S["ident_ready"], 1)
            g.affine_select(out=ident[:, :], in_=ident[:, :], compare_op=ALU.not_equal, fill=1.0, base=0,
                            pattern=[[-1, P]], channel_multiplier=1).then_inc(S["ident_ready"], 1)
            SETUP = 5
            link = Link(pool, S["pool_link"])
            pool.wait_ge(S["vecs"], 160)
            pool.wait_ge(S["const"], 1)
            pool.wait_ge(S["hb_sq"], 1)
            pool.nop(nofuse=True)
            link(g.tensor_scalar(hbs[:, 1:2], hbs[:, 0:1], MIN_NORM2, None, ALU.max))
            link(g.tensor_tensor(hbs[:, 2:3], hbs[:, 1:2], NHALF[:, 0:1], ALU.pow))
            g.tensor_tensor(hbs[:, 3:4], hbs[:, 1:2], hbs[:, 2:3], ALU.mult).then_inc(S["hb_norm"], 1)
            pool.wait_ge(S["hb_tanh"], 1)
            pool.nop(nofuse=True)
            link(g.tensor_scalar(hbs[:, 4:5], hbs[:, 4:5], MAX_NORM, None, ALU.min))
            link(g.tensor_tensor(hbs[:, 4:5], hbs[:, 4:5], hbs[:, 2:3], ALU.mult))
            link(g.tensor_tensor(HB[:, :], HB[:, :], hbs[:, 4:5].to_broadcast([P, P]), ALU.mult))
            g.tensor_tensor(HBC[:, :], HBC[:, :], hbs[:, 4:5], ALU.mult).then_inc(S["hb_ready"], 1)
            assert link.n == SETUP
            def rstd(q, k):
                pool.wait_ge(S["pre_stats"], q + 1)
                pool.nop(nofuse=True)
                Link(pool, S["rstd_link"], q, nop=True)(
                    g.tensor_scalar(r[("v", "t")[k]], (MV, MV2)[k][:, :, 1], LN_EPS, None, ALU.add))
                g.tensor_tensor(r[("rs", "rs2")[k]], r[("v", "t")[k]], NHALF[:, 0:BLK], ALU.pow).then_inc(S["pre_rs"], 1)

            def shift(q, side, i):
                pool.wait_ge(S["pre_scaled"], q + 1)
                if not isinstance(q, int) or q >= 2 * PB:
                    pool.wait_ge(S["xgl"], q - 2 * PB + 1)
                g.tensor_tensor(v4(norm_rows(side, i)), v4((TH, X1)[par(side, i)][:, :]), b4(BIN[:, :]),
                                ALU.add).then_inc(S["pre_xn"], 1)

            def main(q0, side, batch):
                rstd(q0, par(side, 0))
                for i in range(PB):
                    if i + 1 < PB:
                        rstd(q0 + i + 1, par(side, i + 1))
                    shift(q0 + i, side, i)
            prelude(pool, main)

            def atanh_begin(link, k, n2, clip, tc_sem):
                n, i, t, ser, mask = (r[f"{name}_{k}"] for name in ("n2", "inv", "t", "ser", "mask"))
                link(g.tensor_scalar(n, n2, MIN_NORM2, None, ALU.max))
                link(g.tensor_tensor(i, n, NHALF[:, 0:BLK], ALU.pow))
                link(g.tensor_tensor(t, n, i, ALU.mult))
                g.tensor_scalar(r[f"tc_{k}"], t, clip, None, ALU.min).then_inc(S[tc_sem], 1)
                link(g.tensor_scalar(ser, n, 0.2, 1.0 / 3.0, ALU.mult, ALU.add))
                link(g.tensor_tensor(ser, ser, n, ALU.mult))
                link(g.tensor_scalar(ser, ser, 1.0, None, ALU.add))
                link(g.tensor_scalar(mask, n, SERIES_BELOW2, None, ALU.is_lt))

            def atanh_end(link, k, e, ln_sem, k_out):
                la, lb, i, ser, mask = (r[f"{name}_{k}"] for name in ("la", "lb", "inv", "ser", "mask"))
                pool.wait_ge(S[ln_sem], e + 1)
                link(g.tensor_tensor(la, la, lb, ALU.subtract))
                link(g.tensor_tensor(la, la, i, ALU.mult))
                link(g.tensor_scalar(la, la, 0.5, None, ALU.mult))
                link(g.tensor_tensor(ser, ser, la, ALU.subtract))
                link(g.tensor_tensor(ser, ser, mask, ALU.mult))
                return g.tensor_tensor(k_out, ser, la, ALU.add)

            KF, KB = 18, 29

            def chunk_ends(front, back):
                if front is not None:
                    flink = Link(pool, S["front_link"], KF * front, nop=True)
                if back is not None:
                    blink = link = Link(pool, S["back_link"], KB * back, nop=True)
                    pool.wait_ge(S["sq1"], back + 1)
                    pool.nop(nofuse=True)
                    link(g.tensor_scalar(r["n2"], r["m2"], MIN_NORM2, None, ALU.max))
                    link(g.tensor_tensor(r["minv"], r["n2"], NHALF[:, 0:BLK], ALU.pow))
                    link(g.tensor_tensor(r["t"], r["n2"], r["minv"], ALU.mult))
                    g.tensor_tensor(r["q"], r["t"], r["fx"], ALU.mult).then_inc(S["q"], 1)
                    pool.wait_ge(S["tq"], back + 1)
                    pool.nop(nofuse=True)
                    link(g.tensor_scalar(r["tq"], r["tq"], MAX_NORM, None, ALU.min))
                    link(g.tensor_tensor(r["rsc"], r["tq"], r["minv"], ALU.mult))
                    link(g.tensor_tensor(r["x2"], r["rsc"], r["rsc"], ALU.mult))
                    link(g.tensor_tensor(r["x2"], r["x2"], r["m2"], ALU.mult))
                    link(g.tensor_tensor(r["xy"], r["rsc"], r["pxy"], ALU.mult))
                    link(g.tensor_scalar(r["xy"], r["xy"], 2.0, 1.0, ALU.mult, ALU.add))
                    link(g.tensor_tensor(r["a"], r["xy"], y2[:, 0:1].to_broadcast([P, BLK]), ALU.add))
                    link(g.tensor_scalar(r["b"], r["x2"], -1.0, 1.0, ALU.mult, ALU.add))
                    link(g.tensor_tensor(r["den"], r["x2"], y2[:, 0:1].to_broadcast([P, BLK]), ALU.mult))
                    link(g.tensor_tensor(r["den"], r["den"], r["xy"], ALU.add))
                    link(g.tensor_scalar(r["den"], r["den"], MIN_NORM, None, ALU.max))
                    link(g.tensor_tensor(r["den"], r["den"], NEG1[:, :], ALU.pow))
                    link(g.tensor_tensor(r["beta"], r["b"], r["den"], ALU.mult))
                    link(g.tensor_tensor(r["a"], r["a"], r["den"], ALU.mult))
                    g.tensor_tensor(r["alpha"], r["a"], r["rsc"], ALU.mult).then_inc(S["alphabeta"], 1)
                if front is not None:
                    pool.wait_ge(S["stats1"], front + 1)
                    pool.nop(nofuse=True)
                    flink(g.tensor_scalar(r["v"], MV[:, :, 1], LN_EPS, None, ALU.add))
                    g.tensor_tensor(r["rs"], r["v"], NHALF[:, 0:BLK], ALU.pow).then_inc(S["rs1"], 1)
                    g.tensor_tensor(v4(XR[:, :]), v4(XR[:, :]), b4(BOUT[:, :]), ALU.add).then_inc(S["xb"], 1)
                if back is not None:
                    pool.wait_ge(S["sq2"], back + 1)
                    pool.nop(nofuse=True)
                    atanh_begin(blink, 2, r["h2"], MAX_NORM, "tc2")
                if front is not None:
                    pool.wait_ge(S["stats2"], front + 1)
                    pool.nop(nofuse=True)
                    flink(g.tensor_scalar(r["v"], MV2[:, :, 1], LN_EPS, None, ALU.add))
                    g.tensor_tensor(r["rs2"], r["v"], NHALF[:, 0:BLK], ALU.pow).then_inc(S["rs2"], 1)
                    pool.wait_ge(S["rs2"], front + 1)
                    flink(g.tensor_tensor(r["sq"], r["rs2"], r["rs2"], ALU.mult))
                    flink(g.tensor_tensor(r["sq"], r["sq"], MV2[:, :, 1], ALU.mult))
                    flink(g.tensor_scalar(r["sq"], r["sq"], float(P), None, ALU.mult))
                    atanh_begin(flink, 1, r["sq"], ATANH_CLIP, "tc1")
                if back is not None:
                    atanh_end(blink, 2, back, "ln2", r["kap"]).then_inc(S["kap"], 1)
                    assert blink.n == KB, blink.n
                if front is not None:
                    flink(atanh_end(flink, 1, front, "ln1", r["fx"]))
                    pool.wait_ge(S["x1_ready"], front + 1)
                    pool.nop(nofuse=True)
                    pool.dma_start(x1_dram[bass.ds(front * P, P), :], X1[:, :]).then_inc(S["x1_stored"], 16)
                    pool.wait_ge(S["x1_stored"], 16 * (front + 1))
                    assert flink.n == KF, flink.n

            KR = 10

            def result1(e):
                link = Link(pool, S["result_link"], KR * e, nop=True)
                pool.dma_start(XR[:, :], x1_dram[bass.ds(e * P, P), :]).then_inc(S["x1_back"], 16)
                pool.wait_ge(S["sq3"], e + 1)
                pool.nop(nofuse=True)
                link(g.tensor_scalar(r["s2"], r["s2"], MIN_NORM2, None, ALU.max))
                link(g.tensor_tensor(r["w"], r["s2"], NHALF[:, 0:BLK], ALU.pow))
                link(g.tensor_scalar(r["w"], r["w"], ATANH_MAX_NORM, None, ALU.mult))
                link(g.tensor_scalar(r["w"], r["w"], 1.0, None, ALU.min))
                link(g.tensor_scalar(r["r2"], r["r2"], MIN_NORM2, None, ALU.max))
                link(g.tensor_tensor(r["nr"], r["r2"], NHALF[:, 0:BLK], ALU.pow))
                link(g.tensor_tensor(r["nr"], r["nr"], r["r2"], ALU.mult))
                link(g.tensor_tensor(r["nr"], r["nr"], r["w"], ALU.mult))
                g.tensor_scalar(r["t"], r["nr"], MIN_NORM, None, ALU.max).then_inc(S["n3"], 1)
                pool.wait_ge(S["n3"], e + 1)
                link(g.tensor_tensor(r["cf"], r["t"], NEG1[:, :], ALU.pow))
                pool.wait_ge(S["th3"], e + 1)
                pool.nop(nofuse=True)
                link(g.tensor_scalar(r["thn"], r["thn"], MAX_NORM, None, ALU.min))
                g.tensor_tensor(r["cf"], r["cf"], r["thn"], ALU.mult).then_inc(S["coef"], 1)
                pool.wait_ge(S["coef"], 2 * e + 1)
                g.tensor_tensor(r["coef"], r["cf"], r["w"], ALU.mult).then_inc(S["coef"], 1)
                assert link.n == KR, link.n

            def result2(e):
                pool.wait_ge(S["stats3"], e + 1)
                pool.nop(nofuse=True)
                g.tensor_scalar(r["v"], MV[:, :, 1], LN_EPS, None, ALU.add).then_inc(S["rs3"], 1)
                pool.wait_ge(S["rs3"], 2 * e + 1)
                g.tensor_tensor(r["rs"], r["v"], NHALF[:, 0:BLK], ALU.pow).then_inc(S["rs3"], 1)

            def store(e):
                pool.wait_ge(S["res"], e + 1)
                pool.nop(nofuse=True)
                pool.dma_start(out[bass.ds(e * P, P), :], X1[:, :]).then_inc(S["res_stored"], 16)
                pool.wait_ge(S["res_stored"], 16 * (e + 1))

            pool.wait_ge(S["y2_ready"], 1)
            chunk_ends(0, None)
            with pool.Fori(2, NCH + 1) as c:
                chunk_ends(c - 1, c - 2)
            chunk_ends(None, NCH - 1)
            result1(0)
            with pool.Fori(1, NCH) as e:
                result2(e - 1)
                store(e - 1)
                result1(e)
            result2(NCH - 1)
            store(NCH - 1)

        @block.scalar
        def _(act):
            a = nc.scalar
            r = {k: v[:, :] for k, v in small.items()}
            act.wait_ge(S["gum1"], 1)
            a.activation(U[:, :], U[:, :], ACT.Ln).then_inc(S["gum2"], 1)
            act.wait_ge(S["gum1"], 2)
            a.activation(U[:, :], U[:, :], ACT.Ln).then_inc(S["gum2"], 1)
            act.wait_ge(S["vecs"], 160)
            a.activation(JUNK[:, 0:P], HB[:, :], ACT.Square, accum_out=hbs[:, 0:1]).then_inc(S["hb_sq"], 1)
            act.wait_ge(S["hb_norm"], 1)
            a.activation(hbs[:, 4:5], hbs[:, 3:4], ACT.Tanh).then_inc(S["hb_tanh"], 1)
            act.wait_ge(S["hb_ready"], 1)
            a.activation(JUNK[:, 0:P], HB[:, :], ACT.Square, accum_out=y2[:, 0:1]).then_inc(S["y2_ready"], 1)
            act.wait_ge(S["rm_psum"], 1)
            a.activation(RM[:, :], E[:, 3, 0:P + 1], ACT.Copy).then_inc(S["rm_ready"], 1)

            def scale(q, side, i):
                k = par(side, i)
                act.wait_ge(S["pre_rs"], q + 1)
                act.wait_ge(S["pre_z"], q + 1)
                for t in range(BLK):
                    last = a.activation((TH, X1)[k][:, blk(t)], (TH, X1)[k][:, blk(t)], ACT.Copy,
                                        scale=small[("rs", "rs2")[k]][:, t:t + 1])
                last.then_inc(S["pre_scaled"], 1)

            def transposed(q, side, i, batch):
                k = par(side, i)
                act.wait_ge(S["pre_tr"], q + 1)
                wait_n(act, f"xnt_stored{k}", 8 * PB * (batch - side) + 16 * ((PB * side + i) // 2))
                if not isinstance(q, int) or q >= 2:
                    act.wait_ge(S["pre_logit"], q - 1)
                a.activation((XNT, X1T)[k][:, :], E[:, 2 * k, :], ACT.Copy).then_inc(S["pre_xt"], 1)

            def main(q0, side, batch):
                scale(q0, side, 0)
                for i in range(PB):
                    if i + 1 < PB:
                        scale(q0 + i + 1, side, i + 1)
                    transposed(q0 + i, side, i, batch)

            def gates(b, side):
                rows = bass.ds(b * PB * BLK, PB * BLK)
                act.wait_ge(S["gate_arg"], b + 1)
                a.activation(LG[:, rows, :], LG[:, rows, :], ACT.Exp).then_inc(S["gate_exp"], 1)
                for i in range(PB):
                    q = b * PB + i
                    act.wait_ge(S["gated"], q + 1)
                    a.activation(XGH[:, bass.ds(q * CW, CW)], norm_rows(side, i), ACT.Copy).then_inc(S["xgh"], 1)
            prelude(act, main, gates)
            act.wait_ge(S["gate_tr"], 1)
            a.activation(GATET[:, :], E[0:NB, 3, 0:P], ACT.Copy).then_inc(S["gate_rows"], 1)

            def split_high(step, j, k, h):
                if h == 0:
                    turns = (step.n0 + k - k % RING) // RING if isinstance(step.n0, int) else (step.n0 >> 2) + k // RING
                    act.wait_ge(S[f"ld{k % RING}"], 16 * (turns + 1))
                n = 2 * step.n0 + j
                if not (isinstance(n, int) and n < SPLITS):
                    act.wait_ge(S["used"], n - SPLITS + 1)
                a.activation(AH[:, j % SPLITS, :], A[:, k % RING, h * HW:(h + 1) * HW], ACT.Copy).then_inc(S["hi"], 1)

            def lns(k, e, tc_sem, ln_sem):
                act.wait_ge(S[tc_sem], e + 1)
                a.activation(r[f"la_{k}"], r[f"tc_{k}"], ACT.Ln, bias=1.0, scale=1.0)
                a.activation(r[f"lb_{k}"], r[f"tc_{k}"], ACT.Ln, bias=1.0, scale=-1.0).then_inc(S[ln_sem], 1)

            def chunk_ends(j, front, back):
                if j == MX_OUT and back is not None:
                    act.wait_ge(S["mx"], back + 1)
                    a.activation(v4(HY[:, :]), E[:, :, 0:P], ACT.Copy)
                    for t in range(BLK):
                        a.activation(JUNK[:, blk(t)], E[:, t, 0:P], ACT.Square, accum_out=small["m2"][:, t:t + 1])
                    a.activation(r["pxy"], E[:, :, P], ACT.Copy).then_inc(S["sq1"], 1)
                if j == TQ and back is not None:
                    act.wait_ge(S["q"], back + 1)
                    a.activation(r["tq"], r["q"], ACT.Tanh).then_inc(S["tq"], 1)
                if j == TANH and front is not None:
                    act.wait_ge(S["l0_mm"], front + 1)
                    a.activation(v4(TH[:, :]), E[:, :, 0:P], ACT.Tanh, scale=0.5).then_inc(S["tanh"], 1)
                if j == SCALE and back is not None:
                    act.wait_ge(S["alphabeta"], back + 1)
                    for t in range(BLK):
                        a.activation(HY[:, blk(t)], HY[:, blk(t)], ACT.Copy,
                                     scale=small["alpha"][:, t:t + 1]).then_inc(S["scaled"], 1)
                if j == SQ2 and back is not None:
                    act.wait_ge(S["h"], back + 1)
                    for t in range(BLK):
                        last = a.activation(JUNK[:, blk(t)], HY[:, blk(t)], ACT.Square, accum_out=small["h2"][:, t:t + 1])
                    last.then_inc(S["sq2"], 1)
                if j == LN:
                    if back is not None:
                        lns(2, back, "tc2", "ln2")
                    if front is not None:
                        lns(1, front, "tc1", "ln1")
                if j == XT and back is not None:
                    act.wait_ge(S["kap"], back + 1)
                    for t in range(BLK):
                        a.activation(XTH[:, bass.ds(back * CW + t * P, P)], HY[:, blk(t)], ACT.Copy,
                                     scale=small["kap"][:, t:t + 1]).then_inc(S["xth"], 1)
                if j == X1T_AT and front is not None:
                    act.wait_ge(S["x1_tr"], front + 1)
                    a.activation(X1T[:, :], E[:, 0, :], ACT.Copy).then_inc(S["x1t"], 1)

            def result(event, e):
                if event == "relu":
                    act.wait_ge(S["s2_tr"], e + 1)
                    a.activation(TH[:, :], E[:, 0, :], ACT.Relu).then_inc(S["act_link"], 1)
                    for t in range(BLK):
                        a.activation(JUNK[:, blk(t)], E[:, 0, blk(t)], ACT.Square, accum_out=small["s2"][:, t:t + 1])
                    act.wait_ge(S["act_link"], e + 1)
                    for t in range(BLK):
                        last = a.activation(X1T[:, blk(t)], TH[:, blk(t)], ACT.Square, accum_out=small["r2"][:, t:t + 1])
                    last.then_inc(S["sq3"], 1)
                if event == "tanh":
                    act.wait_ge(S["n3"], e + 1)
                    a.activation(r["thn"], r["t"], ACT.Tanh).then_inc(S["th3"], 1)

            def body(step):
                for j, k, h, d, q in step.halves():
                    split_high(step, j, k, h)
                    chunk_ends(j, step.front, step.back)
                    for event, e, _ in results(step, j):
                        result(event, e)
            steps(act, body)
            for event, e in tail():
                result(event, e)

        @block.vector
        def _(dve):
            v = nc.vector
            r = {k: t[:, :] for k, t in small.items()}
            link = Link(dve, S["dve_link"])
            dve.wait_ge(S["urow"], 16)
            v.tensor_scalar(U[:, :], U[:, :], U_EPS, 1.0, ALU.max, ALU.min).then_inc(S["gum1"], 1)
            dve.wait_ge(S["gum2"], 1)
            v.tensor_scalar(U[:, :], U[:, :], -1.0, U_EPS, ALU.mult, ALU.add).then_inc(S["gum1"], 1)
            dve.wait_ge(S["weights"], 16 * 7)
            v.tensor_scalar(RX[:, P:2 * P], RX[:, P:2 * P], 0.5, None, ALU.mult)
            v.tensor_scalar(RS[:, P:2 * P], RS[:, P:2 * P], -0.5, None, ALU.mult).then_inc(S["wt_scaled"], 1)
            dve.wait_ge(S["vecs"], 160)
            dve.wait_ge(S["const"], 1)
            link(v.tensor_tensor(B3[:, P:2 * P], B3[:, P:2 * P], B3[:, 2 * P:3 * P], ALU.subtract))
            link(v.tensor_scalar(B3[:, P:2 * P], B3[:, P:2 * P], 0.5, None, ALU.mult))
            for row in (0, 32):
                v.tensor_copy(BP[row:row + 1, :], B3[row:row + 1, :])
                link(v.tensor_copy(BR[:, :], B3[:, :]))
                link(v.tensor_tensor(B3[:, :], B3[:, :], BR[:, :], ALU.subtract))
            v.tensor_copy(BP[64:65, :], B3[64:65, :]).then_inc(S["bias_ready"], 1)
            if first_low < NCH:
                v.memset(PART[:, 0, :], 0.0)

            def stats(src, mv, done):
                for t in range(BLK):
                    last = v.bn_stats(BS[:, t, :], src[:, blk(t)])
                link(last)
                dve.nop(nofuse=True)
                for t in range(BLK):
                    last = v.bn_aggr(mv[:, t, :], BS[:, t, :])
                last.then_inc(S[done], 1)

            SETUP = link.n
            assert SETUP == 6

            def main(q0, side, batch):
                nonlocal link
                for i in range(PB):
                    q, k, buf = q0 + i, par(side, i), (XR, FU, GB)[i]
                    link = Link(dve, S["stats_link"], q)
                    dve.wait_ge(S[f"xin{i}"], 16 * (batch + 1))
                    if not isinstance(q, int) or q >= 2:
                        dve.wait_ge(S["pre_rs"], q - 1)
                        dve.wait_ge(S["pre_xn"], q - 1)
                    stats(buf, (MV, MV2)[k], "pre_stats")
                    dve.wait_ge(S["pre_stats"], q + 1)
                    for t in range(BLK):
                        last = v.scalar_tensor_tensor(out=(TH, X1)[k][:, blk(t)], in0=buf[:, blk(t)],
                                                      scalar=(MV, MV2)[k][:, t, 0:1], in1=GIN[:, :],
                                                      op0=ALU.subtract, op1=ALU.mult)
                    last.then_inc(S["pre_z"], 1)

            KG = 7

            def gates(b, side):
                link = Link(dve, S["gate_link"], KG * b)
                rows, cols = bass.ds(b * PB * BLK, PB * BLK), bass.ds(b * PB * BLK * 2, PB * BLK * 2)
                dve.wait_ge(S["gum2"], 2)
                dve.wait_ge(S["pre_logit"], PB * (b + 1))
                link(v.scalar_tensor_tensor(out=LG[:, rows, :].rearrange("p b k -> p (b k)"), in0=U[:, cols],
                                            scalar=-1.0, in1=E[:, 1 + 2 * side, cols], op0=ALU.mult, op1=ALU.add))
                link(v.tensor_tensor(LG[:, rows, :], LG[:, rows, :], BNB[:, :].rearrange("p (o k) -> p o k", o=1)
                                     .to_broadcast([P, PB * BLK, 2]), ALU.add))
                link(v.tensor_tensor(TOP[:, rows], LG[:, rows, 0], LG[:, rows, 1], ALU.max))
                v.tensor_tensor(LG[:, rows, 0], LG[:, rows, 0], TOP[:, rows], ALU.subtract)
                v.tensor_tensor(LG[:, rows, 1], LG[:, rows, 1], TOP[:, rows], ALU.subtract).then_inc(S["gate_arg"], 1)
                dve.wait_ge(S["gate_exp"], b + 1)
                link(v.tensor_tensor(SM[:, rows], LG[:, rows, 0], LG[:, rows, 1], ALU.add))
                link(v.reciprocal(SM[:, rows], SM[:, rows]))
                v.tensor_tensor(LG[:, rows, 0], LG[:, rows, 0], SM[:, rows], ALU.mult)
                link(v.tensor_tensor(LG[:, rows, 1], LG[:, rows, 1], SM[:, rows], ALU.mult))
                v.tensor_tensor(TOP[:, rows], LG[:, rows, 1], LG[:, rows, 0], ALU.is_gt).then_inc(S["gate_hard"], 1)
                dve.wait_ge(S["gate_hard"], b + 1)
                link(v.tensor_tensor(TOP[:, rows], TOP[:, rows], LG[:, rows, 1], ALU.add))
                v.tensor_tensor(GATE[:, rows], TOP[:, rows], LG[:, rows, 1], ALU.subtract).then_inc(S["gates"], 1)
                dve.wait_ge(S["gates"], b + 1)
                for i in range(PB):
                    q = b * PB + i
                    x4 = v4(norm_rows(side, i))
                    v.tensor_tensor(x4, x4, GATE[:, bass.ds(q * BLK, BLK)].rearrange("p (b o) -> p b o", o=1)
                                    .to_broadcast([P, BLK, P]), ALU.mult).then_inc(S["gated"], 1)
                for i in range(PB):
                    q = b * PB + i
                    cols = bass.ds(q * CW, CW)
                    dve.wait_ge(S["xgh"], q + 1)
                    v.tensor_tensor(XGL[:, cols], norm_rows(side, i), XGH[:, cols].bitcast(F32),
                                    ALU.subtract).then_inc(S["xgl"], 1)
                assert link.n == KG, link.n
            prelude(dve, main, gates)
            DONE = SETUP

            def split_low(step, j, k, h):
                dve.wait_ge(S["hi"], 2 * step.n0 + j + 1)
                v.tensor_tensor(AL[:, j % SPLITS, :], A[:, k % RING, h * HW:(h + 1) * HW],
                                AH[:, j % SPLITS, :].bitcast(F32), ALU.subtract).then_inc(S["lo"], 1)

            K1 = 6

            def chunk_ends(j, front, back, complete):
                if j == GATED and front is not None:
                    dve.wait_ge(S["used"], complete)
                    dve.wait_ge(S["epi_in"], 48 * (front + 1))
                    v.tensor_tensor(GB[:, :], ACC[:, bass.ds((front % 2) * CW, CW)], GB[:, :],
                                    ALU.mult).then_inc(S["s1_gated"], 1)
                if j == FUSE and front is not None:
                    dve.wait_ge(S["tanh"], front + 1)
                    link(v.scalar_tensor_tensor(out=v4(FU[:, :]), in0=v4(TH[:, :]), scalar=1.0,
                                                in1=E[:, :, P:2 * P], op0=ALU.add, op1=ALU.mult))
                    link(v.tensor_tensor(v4(FU[:, :]), v4(FU[:, :]), E[:, :, 2 * P:3 * P], ALU.add))
                    link(v.tensor_tensor(FU[:, :], FU[:, :], XR[:, :], ALU.add))
                if j == STATS1 and front is not None:
                    stats(FU, MV, "stats1")
                if j == H_AT and back is not None:
                    for t in range(BLK):
                        dve.wait_ge(S["scaled"], BLK * back + t + 1)
                        last = v.scalar_tensor_tensor(out=HY[:, blk(t)], in0=HB[:, :],
                                                      scalar=small["beta"][:, t:t + 1], in1=HY[:, blk(t)],
                                                      op0=ALU.mult, op1=ALU.add)
                    last.then_inc(S["h"], 1)
                if j == CENTER and front is not None:
                    dve.wait_ge(S["rs1"], front + 1)
                    for t in range(BLK):
                        last = v.scalar_tensor_tensor(out=FU[:, blk(t)], in0=FU[:, blk(t)], scalar=MV[:, t, 0:1],
                                                      in1=GOUT[:, :], op0=ALU.subtract, op1=ALU.mult)
                    last.then_inc(S["centered"], 1)
                    dve.wait_ge(S["centered"], front + 1)
                    dve.wait_ge(S["xb"], front + 1)
                    for t in range(BLK):
                        last = v.scalar_tensor_tensor(out=FU[:, blk(t)], in0=FU[:, blk(t)],
                                                      scalar=small["rs"][:, t:t + 1], in1=XR[:, blk(t)],
                                                      op0=ALU.mult, op1=ALU.add)
                    link(last)
                if j == STATS2 and front is not None:
                    stats(FU, MV2, "stats2")
                if j == X1_AT and front is not None:
                    dve.wait_ge(S["rs2"], front + 1)
                    for t in range(BLK):
                        last = v.tensor_scalar(X1[:, blk(t)], FU[:, blk(t)], MV2[:, t, 0:1],
                                               small["rs2"][:, t:t + 1], ALU.subtract, ALU.mult)
                    last.then_inc(S["x1_ready"], 1)
                if j == XT and back is not None:
                    for t in range(BLK):
                        cols = bass.ds(back * CW + t * P, P)
                        dve.wait_ge(S["xth"], BLK * back + t + 1)
                        last = v.scalar_tensor_tensor(out=XTL[:, cols], in0=HY[:, blk(t)],
                                                      scalar=small["kap"][:, t:t + 1], in1=XTH[:, cols].bitcast(F32),
                                                      op0=ALU.mult, op1=ALU.subtract)
                    last.then_inc(S["xtl"], 1)

            K3, STATS_LINKS = 2, NCH

            def result(event, e, complete, with_part):
                nonlocal link
                if event == "take":
                    dve.wait_ge(S["used"], complete)
                    acc = ACC[:, bass.ds((e % 4) * CW, CW)]
                    if with_part:
                        v.tensor_tensor(GB[:, :], acc, PART[:, e - (first_low - 1), :], ALU.add).then_inc(S["s2_taken"], 1)
                    else:
                        v.tensor_copy(GB[:, :], acc).then_inc(S["s2_taken"], 1)
                if event == "add":
                    link = Link(dve, S["stats_link"], STATS_LINKS + K3 * e)
                    dve.wait_ge(S["coef"], 2 * e + 2)
                    dve.wait_ge(S["x1_back"], 16 * (e + 1))
                    for t in range(BLK):
                        last = v.scalar_tensor_tensor(out=FU[:, blk(t)], in0=TH[:, blk(t)],
                                                      scalar=small["coef"][:, t:t + 1], in1=XR[:, blk(t)],
                                                      op0=ALU.mult, op1=ALU.add)
                    link(last)
                    stats(FU, MV, "stats3")
                    assert link.n == K3
                if event == "norm":
                    dve.wait_ge(S["rs3"], 2 * e + 2)
                    for t in range(BLK):
                        last = v.tensor_scalar(X1[:, blk(t)], FU[:, blk(t)], MV[:, t, 0:1],
                                               small["rs"][:, t:t + 1], ALU.subtract, ALU.mult)
                    last.then_inc(S["res"], 1)

            def body(step):
                nonlocal link
                if step.front is not None:
                    link = Link(dve, S["dve_link"], DONE + K1 * step.front)
                for j, k, h, d, q in step.halves():
                    split_low(step, j, k, h)
                    if step.phase == 1 and step.lw and j == min(2 * step.lw + SPLITS - 1, 2 * NCH - 1):
                        dve.wait_ge(S["used"], 2 * (step.n0 + step.lw))
                        v.tensor_copy(PART[:, step.c - (first_low - 1), :],
                                      ACC[:, bass.ds((step.c % 2) * CW + 2 * CW, CW)]).then_inc(S["part_saved"], 1)
                    chunk_ends(j, step.front, step.back, 2 * step.n0)
                    for event, e, complete in results(step, j):
                        result(event, e, complete, step.lw > 0)
                if step.front is not None:
                    assert link.n == K1, link.n
            steps(dve, body)
            for event, e in tail():
                result(event, e, 2 * TOTAL, True)

        @block.tensor
        def _(pe):
            p = nc.tensor
            pe.wait_ge(S["weights"], 16 * 7)
            pe.wait_ge(S["ident_ready"], 2)
            pe.wait_ge(S["hb_ready"], 1)
            p.transpose(E[:, 3, 0:P], WH[:, :], ident[:, :])
            p.matmul(E[:, 3, P:P + 1], WH[:, :], HBC[:, :], start=True, stop=True).then_inc(S["rm_psum"], 1)
            pe.wait_ge(S["rm_ready"], 1)
            def transposes(q, side, i):
                pe.wait_ge(S["pre_xn"], q + 1)
                if not isinstance(q, int) or q >= 2:
                    pe.wait_ge(S["pre_xt"], q - 1)
                for t in range(BLK):
                    last = p.transpose(E[:, 2 * par(side, i), blk(t)], norm_rows(side, i)[:, blk(t)], ident[:, :])
                last.then_inc(S["pre_tr"], 1)

            def logits(q, side, i):
                xt = (XNT, X1T)[par(side, i)]
                pe.wait_ge(S["pre_xt"], q + 1)
                for t in range(BLK):
                    last = p.matmul(E[:, 1 + 2 * side, bass.ds(q * 2 * BLK + 2 * t, 2)], xt[:, blk(t)], WN[:, :],
                                    start=True, stop=True)
                last.then_inc(S["pre_logit"], 1)

            def main(q0, side, batch):
                transposes(q0, side, 0)
                if not isinstance(batch, int) or batch >= 2:
                    pe.wait_ge(S["gate_arg"], batch - 1)
                for i in range(PB):
                    if i + 1 < PB:
                        transposes(q0 + i + 1, side, i + 1)
                    logits(q0 + i, side, i)
            prelude(pe, main)
            pe.wait_ge(S["gates"], NCH // PB)
            p.transpose(E[0:NB, 3, 0:P], GATE[:, :], ident[:, :]).then_inc(S["gate_tr"], 1)

            def chunk_ends(j, front, back):
                if front is not None and L0 <= j < L0 + BLK:
                    if j == L0:
                        pe.wait_ge(S["s1_gated"], front + 1)
                        pe.wait_ge(S["epi_in"], 48 * (front + 1))
                        if back is not None:
                            pe.wait_ge(S["sq1"], back + 1)
                    t = j - L0
                    p.matmul(E[:, t, 0:3 * P], ones[:, :], BP[:, :], start=True, stop=False)
                    p.matmul(E[:, t, 0:2 * P], XNT[:, blk(t)], RX[:, :], start=False, stop=False)
                    last = p.matmul(E[:, t, 0:3 * P], GB[:, blk(t)], RS[:, :], start=False, stop=True)
                    if t == BLK - 1:
                        last.then_inc(S["l0_mm"], 1)
                if front is not None and j == X1_TR:
                    pe.wait_ge(S["x1_ready"], front + 1)
                    for t in range(BLK):
                        last = p.transpose(E[:, 0, blk(t)], X1[:, blk(t)], ident[:, :])
                    last.then_inc(S["x1_tr"], 1)
                if front is not None and j == MX:
                    pe.wait_ge(S["x1t"], front + 1)
                    for t in range(BLK):
                        last = p.matmul(E[:, t, 0:P + 1], X1T[:, blk(t)], RM[:, :], start=True, stop=True)
                    last.then_inc(S["mx"], 1)

            def three_pass(acc, hi, lo, q, t, j, start, stop):
                st = blk(BLK * q + t)
                mv = slice((t % 2) * CW, (t % 2 + 1) * CW)
                p.matmul(acc, hi[:, st], AH[:, j % SPLITS, mv], start=start, stop=False)
                p.matmul(acc, hi[:, st], AL[:, j % SPLITS, mv], start=False, stop=False)
                return p.matmul(acc, lo[:, st], AH[:, j % SPLITS, mv], start=False, stop=stop)

            def result(event, e):
                if event == "turn":
                    pe.wait_ge(S["s2_taken"], e + 1)
                    for t in range(BLK):
                        last = p.transpose(E[:, 0, blk(t)], GB[:, blk(t)], ident[:, :])
                    last.then_inc(S["s2_tr"], 1)

            def body(step):
                c, lw = step.c, step.lw
                for j, k, h, d, q in step.halves():
                    if step.phase == 1 and isinstance(c, int) and c == 0 and h == 0:
                        pe.wait_ge(S["xgl"], q + 1)
                    if step.phase == 1 and q < lw and h == 0:
                        pe.wait_ge(S["xtl"], q + 1)
                    if step.mixed:
                        if h == 0:
                            pe.wait_ge(S["xtl"], q + 1)
                        if q == 0 and h == 0 and d < 2:
                            pe.wait_ge(S["s1_gated"], NCH - 1 + d)
                        if q == 0 and h == 0 and d == 2 and first_low < NCH:
                            pe.wait_ge(S["part_saved"], NCH - first_low)
                    pe.wait_ge(S["lo"], 2 * step.n0 + j + 1)
                    for t in (2 * h, 2 * h + 1):
                        begin, end = q == (lw if step.phase == 2 else 0) and t == 0, q == NCH - 1 and t == BLK - 1
                        if step.phase == 1:
                            last = three_pass(ACC[:, bass.ds((c % 2) * CW, CW)], XGH, XGL, q, t, j, begin, end)
                            if q < lw:
                                last = three_pass(ACC[:, bass.ds((c % 2) * CW + 2 * CW, CW)], XTH, XTL, q, t, j, begin,
                                                  q == lw - 1 and t == BLK - 1)
                        else:
                            last = three_pass(ACC[:, bass.ds(((c + d) % 4) * CW, CW)], XTH, XTL, q, t, j, begin, end)
                    last.then_inc(S["used"], 1)
                    chunk_ends(j, step.front, step.back)
                    for event, e, _ in results(step, j):
                        result(event, e)
            pe.wait_ge(S["wt_scaled"], 1)
            pe.wait_ge(S["bias_ready"], 1)
            steps(pe, body)
            for event, e in tail():
                result(event, e)


_INS = ["x", "adjT", "u", "w1", "b1", "w2", "b2", "wg", "bg", "wn", "bn", "g_in", "b_in", "g_out", "b_out",
        "w_hyp", "b_hyp"]


def kernel(**inputs):
    import numpy as np
    import concourse.bacc as bacc
    from concourse.bass_utils import run_bass_kernel_spmd as run

    given = {k: np.asarray(v) for k, v in inputs.items()}
    n, d = given["x"].shape
    nch = n // CW
    host = {
        "x": given["x"].reshape(nch, BLK, P, d).transpose(0, 2, 1, 3).reshape(nch * P, CW),
        "adjT": given["adj"].reshape(nch, CW, nch, BLK, P).transpose(0, 2, 4, 3, 1).reshape(nch * nch * P, GW),
        "u": given["L0_gnn_u"].reshape(n // P, P, 2).transpose(1, 0, 2).reshape(P, n // P * 2),
        "w1": given["L0_gnn_W1"], "b1": given["L0_gnn_b1"], "w2": given["L0_gnn_W2"], "b2": given["L0_gnn_b2"],
        "wg": given["L0_gnn_Wg"], "bg": given["L0_gnn_bg"], "wn": given["L0_gnn_Wn"], "bn": given["L0_gnn_bn"],
        "g_in": given["L0_gnn_g_in"], "b_in": given["L0_gnn_b_in"], "g_out": given["L0_gnn_g_out"],
        "b_out": given["L0_gnn_b_out"], "w_hyp": given["L1_gnn_weight"], "b_hyp": given["L1_gnn_bias"],
    }
    nc = bacc.Bacc("TRN2", target_bir_lowering=False, num_devices=1)
    arrays, args = {}, []
    for name in _INS:
        a = np.ascontiguousarray(host[name])
        arrays[f"in_{name}_dram"] = a
        args.append(nc.dram_tensor(f"in_{name}_dram", a.shape, mybir.dt.from_np(a.dtype), kind="ExternalInput").ap())
    args.append(nc.dram_tensor("out_0_dram", (nch * P, CW), F32, kind="ExternalOutput").ap())
    build(nc, *args)
    r = run(nc, [arrays], core_ids=[0])
    got = r.results[0]["out_0_dram"]
    return got.reshape(nch, P, BLK, d).transpose(0, 2, 1, 3).reshape(n, d)
```

```python
from contextlib import ExitStack

import concourse.bass as bass
from concourse import mybir

F32 = mybir.dt.float32
F32R = mybir.dt.float32r
BF16 = mybir.dt.bfloat16
ALU = mybir.AluOpType
ACT = mybir.ActivationFunctionType

P = 128
BLK = 4
CW = BLK * P
GW = BLK * CW
RING = 4
HW = GW // 2
SPLITS = 4
LN_EPS = 1e-5
U_EPS = 1e-10
MIN_NORM = 1e-15
MIN_NORM2 = 1e-30
MAX_NORM = 0.996
ATANH_CLIP = 0.9999998807907104
ATANH_MAX_NORM = 3.1063027
SERIES_BELOW2 = 0.0025


def low(c):
    return RING * ((c - 2) // RING) if c >= 2 else 0


def bands(first, nch):
    out = []
    for c in range(first, nch):
        if out and out[-1][2] == low(c):
            out[-1][1] = c + 1
        else:
            out.append([c, c + 1, low(c)])
    return [tuple(b) for b in out]


def build(nc, x, adjT, u, w1, b1, w2, b2, wg, bg, wn, bn, g_in, b_in, g_out, b_out, w_hyp, b_hyp, out):
    N = x.shape[0] * x.shape[1] // P
    NCH = N // CW
    NB = N // P
    N1 = NCH * NCH
    assert NCH % RING == 0

    with ExitStack() as ctx:
        def sb(name, shape, dt=F32):
            return ctx.enter_context(nc.sbuf_tensor(name, shape, dt))

        def sem(name):
            return ctx.enter_context(nc.semaphore(name))

        A = sb("A", [P, RING, GW])
        AH = sb("AH", [P, SPLITS, HW], F32R)
        AL = sb("AL", [P, SPLITS, HW], F32R)
        XGH = sb("XGH", [P, N], F32R)
        XGL = sb("XGL", [P, N], F32R)
        XTH = sb("XTH", [P, N], F32R)
        XTL = sb("XTL", [P, N], F32R)
        first_low = min([c for c in range(NCH) if low(c)] or [NCH])
        PART = sb("PART", [P, NCH - first_low + 1, CW])
        XR = sb("XR", [P, CW])
        XNT = sb("XNT", [P, CW])
        GB = sb("GB", [P, CW])
        TH = sb("TH", [P, CW])
        FU = sb("FU", [P, CW])
        X1 = sb("X1", [P, CW])
        X1T = sb("X1T", [P, CW])
        HY = sb("HY", [P, CW])
        JUNK = sb("JUNK", [P, CW])
        ident = sb("ident", [P, P])
        RX = sb("RX", [P, 2 * P])
        RS = sb("RS", [P, 3 * P])
        RM = sb("RM", [P, P + 1])
        WH = sb("WH", [P, P])
        WN = sb("WN", [P, 2])
        GIN = sb("GIN", [P, P])
        BIN = sb("BIN", [P, P])
        GOUT = sb("GOUT", [P, P])
        BOUT = sb("BOUT", [P, P])
        HB = sb("HB", [P, P])
        HBC = sb("HBC", [P, 1])
        BNB = sb("BNB", [P, 2])
        B3 = sb("B3", [P, 3 * P])
        BP = sb("BP", [P, 3 * P], BF16)
        BR = sb("BR", [P, 3 * P], BF16)
        ones = sb("ones", [P, P], BF16)
        NHALF = sb("NHALF", [P, NB])
        NEG1 = sb("NEG1", [P, BLK])
        U = sb("U", [P, NB * 2])
        LG = sb("LG", [P, NB, 2])
        TOP = sb("TOP", [P, NB])
        SM = sb("SM", [P, NB])
        GATE = sb("GATE", [P, NB])
        GATET = sb("GATET", [NB, P])
        BS = sb("BS", [P, BLK, 6])
        MV = sb("MV", [P, BLK, 2])
        MV2 = sb("MV2", [P, BLK, 2])
        small = {n: sb("r_" + n, [P, BLK]) for n in (
            "v", "rs", "rs2", "n2", "t", "fx", "m2", "pxy", "minv", "q", "sq", "mm", "cf", "coef",
            "n2_1", "inv_1", "t_1", "tc_1", "la_1", "lb_1", "ser_1", "mask_1",
            "n2_2", "inv_2", "t_2", "tc_2", "la_2", "lb_2", "ser_2", "mask_2",
            "tq", "rsc", "x2", "xy", "a", "b", "den", "alpha", "beta", "h2", "kap", "s2", "r2", "w", "nr", "thn")}
        y2 = sb("y2", [P, 1])
        hbs = sb("hbs", [P, 5])

        ACC = ctx.enter_context(nc.psum_tensor("ACC", [P, 4 * CW], F32))
        E = ctx.enter_context(nc.psum_tensor("E", [P, 4, CW], F32))

        xnt_dram = nc.dram_tensor("xnt_scratch", [NCH * P, CW], F32).ap()
        gate_dram = nc.dram_tensor("gate_scratch", [NCH, CW], F32).ap()
        x1_dram = nc.dram_tensor("x1_scratch", [NCH * P, CW], F32).ap()

        S = {}
        for name in (
                "act_link", "front_link", "rstd_link", "norm_vecs", "minus_mean", "gate_link", "gate_hard", "pre_scaled", "xin2", "back_link", "result_link", "stats_link", "alphabeta", "bias_ready", "centered", "coef", "const", "dve_link",
                "epi_in", "gate_arg", "gate_exp", "gate_rows", "gate_stored", "gate_tr", "gated",
                "gates", "gum1", "gum2", "h", "hb_norm", "hb_ready", "hb_sq", "hb_tanh", "hi",
                "ident_ready", "kap", "l0_mm", "ld0", "ld1", "ld2", "ld3", "ln1", "ln2", "lo", "mx",
                "n3", "part_saved", "pool_link", "pre_logit", "pre_rs", "pre_stats", "pre_tr",
                "pre_xn", "pre_xt", "pre_z", "q", "res", "res_stored", "rm_psum", "rm_ready", "rs1",
                "rs2", "rs3", "s1_gated", "s2_taken", "s2_tr", "scaled", "sq1", "sq2", "sq3",
                "stats1", "stats2", "stats3", "tanh", "tc1", "tc2", "th3", "tq", "urow", "used",
                "vecs", "weights", "wt_scaled", "x1_back", "x1_ready", "x1_stored", "x1_tr", "x1t",
                "xb", "xgh", "xgl", "xin0", "xin1", "xnt_stored0", "xnt_stored1", "xth", "xtl",
                "y2_ready"):
            S[name] = sem("s_" + name)

        block = ctx.enter_context(nc.Block())

        class Link:

            def __init__(self, eng, s, base=0, nop=False):
                self.eng, self.s, self.base, self.nop, self.n = eng, s, base, nop, 0

            def __call__(self, ins):
                self.n += 1
                ins.then_inc(self.s, 1)
                self.eng.wait_ge(self.s, self.base + self.n)
                if self.nop:
                    self.eng.nop(nofuse=True)

        def wait_n(eng, name, value):
            if not (isinstance(value, int) and value <= 0):
                eng.wait_ge(S[name], value)

        def b4(ap):
            return ap.rearrange("p (o d) -> p o d", o=1).to_broadcast([P, BLK, P])

        def v4(ap):
            return ap.rearrange("p (b d) -> p b d", b=BLK)

        def blk(t):
            return slice(t * P, (t + 1) * P)

        PB = 3
        assert NCH % (2 * PB) == 0 and NCH - first_low >= 2 * PB

        def prelude(eng, main, gates=None):
            def pair(h):
                for side in range(2):
                    b = 2 * h + side

                    def between(i):
                        back = 2 if i == 0 else 1
                        if gates and not (isinstance(b, int) and b < back):
                            gates(b - back, (side + back) % 2, i)
                    main(2 * PB * h + PB * side, side, b, between)
            pair(0)
            with eng.Fori(1, NCH // (2 * PB)) as h:
                pair(h)
            if gates:
                gates(NCH // PB - 2, 0, 0)
                for i in (1, 2, 0):
                    gates(NCH // PB - 1, 1, i)

        def norm_rows(side, i):
            return PART[:, 1 + PB * side + i, :]

        ROWS = (TH, X1, HY)

        def par(side, i):
            return (PB * side + i) % 2

        LAST = NCH - 2
        order = ([(0, q) for q in range(LAST)] + [(1, q) for q in range(LAST)] + [(2, q) for q in range(LAST - RING - 2)]
                 + [(0, LAST), (0, LAST + 1), (1, LAST), (1, LAST + 1)]
                 + [(2, q) for q in range(LAST - RING - 2, NCH)])
        assert low(2) == 0 and len(order) == 3 * NCH
        FRONT = 3
        START2 = N1 + FRONT * NCH

        def phase2_base():
            base, n = {}, START2
            for lo_c, hi_c, lw in bands(FRONT, NCH - 2):
                base[lo_c] = n
                n += (hi_c - lo_c) * (NCH - lw)
            return base, n
        BASE2, START_LAST = phase2_base()
        LOW_LAST = low(NCH - 2)
        assert low(NCH - 1) == LOW_LAST and NCH - LOW_LAST == RING
        TOTAL = START_LAST + 2 * RING

        class Step:
            def __init__(self, phase, c, groups, n0, lw=0, front=None, back=None, result1=None, result2=None):
                self.phase, self.c, self.groups, self.n0, self.lw = phase, c, groups, n0, lw
                self.front, self.back = front, back
                self.result1, self.result2 = result1, result2
                self.places = result_places(len(groups))
                self.first = phase == 1 and isinstance(c, int) and c == 0
                self.mixed = phase == 2 and isinstance(c, int)

            def halves(self):
                for k, (d, q) in enumerate(self.groups):
                    for h in range(2):
                        yield 2 * k + h, k, h, d, q

        def steps(eng, body):
            whole = [(0, q) for q in range(NCH)]

            def both_at(lw):
                alone = lw + both_from(lw)
                return whole[lw:alone] + whole[0:lw] + whole[alone:]
            body(Step(1, 0, whole, 0))
            body(Step(1, 1, whole, NCH, front=0))
            for c0, c1, lw in bands(2, NCH):
                with eng.Fori(c0, c1) as c:
                    body(Step(1, c, both_at(lw), NCH * c, lw, front=c - 1, back=c - 2))
            body(Step(2, 0, order[0:NCH], N1, front=NCH - 1, back=NCH - 2))
            body(Step(2, 0, order[NCH:2 * NCH], N1 + NCH, back=NCH - 1))
            body(Step(2, 0, order[2 * NCH:], N1 + 2 * NCH))
            for c0, c1, lw in bands(FRONT, NCH - 2):
                with eng.Fori(c0, c1) as c:
                    body(Step(2, c, [(0, q) for q in range(lw, NCH)], BASE2[c0] + (NCH - lw) * (c - c0), lw,
                              result1=c - 1, result2=c - 2))
            body(Step(2, NCH - 2, [(d, q) for d in range(2) for q in range(LOW_LAST, NCH)], START_LAST, LOW_LAST))

        def at(k):
            return k * NCH // 12
        GATED, L0, TANH, FUSE, STATS1, CENTER, SHIFT, STATS2, X1_AT, X1_TR, LN1, X1T_AT, MX = (
            at(k) for k in (1, 1, 8, 8, 9, 12, 14, 15, 18, 17, 20, 22, 22))
        L0_EVERY = 1

        def both_from(lw):
            return min(at(4), NCH - lw - 2)

        PREPARE, HB_SQ, HB_TANH, HB_Y2, HB_MM, HB_OUT, HB_DONE = (at(k) for k in (2, 2, 6, 10, 10, 16, 20))
        MX_OUT, TQ, SCALE, H_AT, SQ2, LN2, XT = (at(k) for k in (3, 6, 10, 10, 12, 16, 19))

        def result_places(groups):
            last = 2 * groups - 1
            return {"add": 0, "take": 1, "turn": 1, "relu": 5, "norm": 5, "tanh": min(10, last)}

        third = {("take", 0): 5, ("turn", 0): 5, ("relu", 0): 9, ("tanh", 0): 13,
                 ("add", 0): 16, ("take", 1): 17, ("turn", 1): 17, ("relu", 1): 21, ("norm", 0): 20, ("tanh", 1): 23}
        final = {("add", NCH - 4): 0, ("take", NCH - 3): 1, ("turn", NCH - 3): 1, ("relu", NCH - 3): 5,
                 ("norm", NCH - 4): 5, ("tanh", NCH - 3): 9, ("add", NCH - 3): 10, ("take", NCH - 2): 11,
                 ("turn", NCH - 2): 11, ("norm", NCH - 3): 13, ("relu", NCH - 2): 15}
        tables = {N1 + 2 * NCH: third, START_LAST: final}
        used_in = {(N1 + 2 * NCH, 0): 2, (N1 + 2 * NCH, 1): 4, (START_LAST, NCH - 3): 0, (START_LAST, NCH - 2): RING}

        def results(step, j):
            if step.mixed:
                return [(ev, e, 2 * (step.n0 + used_in.get((step.n0, e), 0)))
                        for (ev, e), place in tables.get(step.n0, {}).items() if place == j]
            if step.phase == 1:
                return []
            return [(ev, step.result2 if ev in ("add", "norm") else step.result1, 2 * step.n0)
                    for ev, place in step.places.items() if place == j]

        def tail():
            return [("take", NCH - 1), ("turn", NCH - 1), ("tanh", NCH - 2), ("add", NCH - 2), ("relu", NCH - 1),
                    ("norm", NCH - 2), ("tanh", NCH - 1), ("add", NCH - 1), ("norm", NCH - 1)]

        @block.sync
        def _(sp):
            XIN = (XR, FU, GB)

            def load_x(q, i):
                sp.dma_start(XIN[i][:, :], x[bass.ds(q * P, P), :]).then_inc(S[f"xin{i}"], 16)

            def store_xnt(q, k):
                sp.wait_ge(S["pre_xt"], q + 1)
                sp.dma_start(xnt_dram[bass.ds(q * P, P), :], (XNT, X1T)[k][:, :]).then_inc(S[f"xnt_stored{k}"], 16)
            load_x(0, 0)
            sp.dma_start(U[:, :], u).then_inc(S["urow"], 16)
            for t, v in ((GIN[:, :], g_in), (BIN[:, :], b_in)):
                sp.dma_start(t, v.partition_broadcast(P)).then_inc(S["norm_vecs"], 16)
            load_x(1, 1)
            load_x(2, 2)
            sp.dma_start(WN[:, :], wn).then_inc(S["weights"], 16)
            for t, v in ((GOUT[:, :], g_out), (BOUT[:, :], b_out),
                         (HB[:, :], b_hyp), (B3[:, 0:P], bg), (B3[:, P:2 * P], b1), (B3[:, 2 * P:3 * P], b2),
                         (BNB[:, :], bn)):
                sp.dma_start(t, v.partition_broadcast(P)).then_inc(S["vecs"], 16)
            sp.dma_start(HBC[:, :], b_hyp.rearrange("(p o) -> p o", o=1)).then_inc(S["vecs"], 16)
            sp.dma_start(RX[:, 0:P], wg[0:P, :]).then_inc(S["weights"], 16)
            sp.dma_start(RX[:, P:2 * P], w1).then_inc(S["weights"], 16)
            sp.dma_start(RS[:, 0:P], wg[P:2 * P, :]).then_inc(S["weights"], 16)
            sp.dma_start(RS[:, P:2 * P], w2).then_inc(S["weights"], 16)
            sp.dma_start(RS[:, 2 * P:3 * P], w2).then_inc(S["weights"], 16)
            sp.dma_start(WH[:, :], w_hyp).then_inc(S["weights"], 16)

            def sp_prelude(h, last):
                for side in range(2):
                    for i in range(PB):
                        q = 2 * PB * h + PB * side + i
                        if not (last and side):
                            sp.wait_ge(S["pre_z"], q + 1)
                            load_x(q + PB, i)
                        store_xnt(q, par(side, i))
            with sp.Fori(0, NCH // (2 * PB) - 1) as h:
                sp_prelude(h, False)
            for q in range(RING):
                sp.dma_start(A[:, q, :], adjT[bass.ds(q * P, P), :]).then_inc(S[f"ld{q}"], 16)
            sp_prelude(NCH // (2 * PB) - 1, True)
            sp.wait_ge(S["gate_rows"], 1)
            sp.dma_start(gate_dram.rearrange("c (t p) -> (c t) p", p=P), GATET[:, :]).then_inc(S["gate_stored"], 16)

            def body(step):
                for k, (d, q) in enumerate(step.groups):
                    n = step.n0 + k
                    if isinstance(n, int) and n < RING:
                        continue
                    sp.wait_ge(S["lo"], 2 * (n - RING + 1))
                    sp.dma_start(A[:, k % RING, :],
                                 adjT[bass.ds(((step.c + d) * NCH + q) * P, P), :]).then_inc(S[f"ld{k % RING}"], 16)
                    if k == 0 and step.front is not None:
                        c = step.front
                        if isinstance(c, int) and c == 0:
                            sp.wait_ge(S["gate_stored"], 16)
                            sp.wait_ge(S["xnt_stored0"], 16 * (NCH // 2))
                            sp.wait_ge(S["xnt_stored1"], 16 * (NCH // 2))
                        wait_n(sp, "stats2", c)
                        wait_n(sp, "l0_mm", c)
                        sp.dma_start(GB[:, :], gate_dram[bass.ds(c, 1), :].partition_broadcast(P)
                                     ).then_inc(S["epi_in"], 16)
                        sp.dma_start(XNT[:, :], xnt_dram[bass.ds(c * P, P), :]).then_inc(S["epi_in"], 16)
                        sp.dma_start(XR[:, :], x[bass.ds(c * P, P), :]).then_inc(S["epi_in"], 16)
            steps(sp, body)

        @block.gpsimd
        def _(pool):
            g = nc.gpsimd
            r = {k: v[:, :] for k, v in small.items()}
            g.memset(ident[:, :], 0.0).then_inc(S["ident_ready"], 1)
            g.memset(ones[:, :], 1.0)
            g.memset(NHALF[:, :], -0.5)
            g.memset(NEG1[:, :], -1.0)
            g.memset(BP[:, :], 0.0).then_inc(S["const"], 1)
            pool.wait_ge(S["ident_ready"], 1)
            g.affine_select(out=ident[:, :], in_=ident[:, :], compare_op=ALU.not_equal, fill=1.0, base=0,
                            pattern=[[-1, P]], channel_multiplier=1).then_inc(S["ident_ready"], 1)
            pool.wait_ge(S["const"], 1)
            pool.wait_ge(S["norm_vecs"], 32)
            def rstd(q, k):
                pool.wait_ge(S["pre_stats"], q + 1)
                pool.nop(nofuse=True)
                Link(pool, S["rstd_link"], q, nop=True)(
                    g.tensor_scalar(r[("v", "t")[k]], (MV, MV2)[k][:, :, 1], LN_EPS, None, ALU.add))
                g.tensor_tensor(r[("rs", "rs2")[k]], r[("v", "t")[k]], NHALF[:, 0:BLK], ALU.pow).then_inc(S["pre_rs"], 1)

            def shift(q, side, i):
                pool.wait_ge(S["pre_scaled"], q + 1)
                if not isinstance(q, int) or q >= 2 * PB:
                    pool.wait_ge(S["xgl"], q - 2 * PB + 1)
                g.tensor_tensor(v4(norm_rows(side, i)), v4(ROWS[i][:, :]), b4(BIN[:, :]),
                                ALU.add).then_inc(S["pre_xn"], 1)

            def main(q0, side, batch, between):
                rstd(q0, par(side, 0))
                for i in range(PB):
                    if i + 1 < PB:
                        rstd(q0 + i + 1, par(side, i + 1))
                    shift(q0 + i, side, i)
            prelude(pool, main)

            SETUP = 5
            link = Link(pool, S["pool_link"])
            pool.wait_ge(S["vecs"], 128)
            pool.wait_ge(S["hb_sq"], 1)
            pool.nop(nofuse=True)
            link(g.tensor_scalar(hbs[:, 1:2], hbs[:, 0:1], MIN_NORM2, None, ALU.max))
            link(g.tensor_tensor(hbs[:, 2:3], hbs[:, 1:2], NHALF[:, 0:1], ALU.pow))
            g.tensor_tensor(hbs[:, 3:4], hbs[:, 1:2], hbs[:, 2:3], ALU.mult).then_inc(S["hb_norm"], 1)
            pool.wait_ge(S["hb_tanh"], 1)
            pool.nop(nofuse=True)
            link(g.tensor_scalar(hbs[:, 4:5], hbs[:, 4:5], MAX_NORM, None, ALU.min))
            link(g.tensor_tensor(hbs[:, 4:5], hbs[:, 4:5], hbs[:, 2:3], ALU.mult))
            link(g.tensor_tensor(HB[:, :], HB[:, :], hbs[:, 4:5].to_broadcast([P, P]), ALU.mult))
            g.tensor_tensor(HBC[:, :], HBC[:, :], hbs[:, 4:5], ALU.mult).then_inc(S["hb_ready"], 1)
            assert link.n == SETUP

            def atanh_begin(link, k, n2, clip, tc_sem):
                n, i, t, ser, mask = (r[f"{name}_{k}"] for name in ("n2", "inv", "t", "ser", "mask"))
                link(g.tensor_scalar(n, n2, MIN_NORM2, None, ALU.max))
                link(g.tensor_tensor(i, n, NHALF[:, 0:BLK], ALU.pow))
                link(g.tensor_tensor(t, n, i, ALU.mult))
                g.tensor_scalar(r[f"tc_{k}"], t, clip, None, ALU.min).then_inc(S[tc_sem], 1)
                link(g.tensor_scalar(ser, n, 0.2, 1.0 / 3.0, ALU.mult, ALU.add))
                link(g.tensor_tensor(ser, ser, n, ALU.mult))
                link(g.tensor_scalar(ser, ser, 1.0, None, ALU.add))
                link(g.tensor_scalar(mask, n, SERIES_BELOW2, None, ALU.is_lt))

            def atanh_end(link, k, e, ln_sem, k_out):
                la, lb, i, ser, mask = (r[f"{name}_{k}"] for name in ("la", "lb", "inv", "ser", "mask"))
                pool.wait_ge(S[ln_sem], e + 1)
                link(g.tensor_tensor(la, la, lb, ALU.subtract))
                link(g.tensor_tensor(la, la, i, ALU.mult))
                link(g.tensor_scalar(la, la, 0.5, None, ALU.mult))
                link(g.tensor_tensor(ser, ser, la, ALU.subtract))
                link(g.tensor_tensor(ser, ser, mask, ALU.mult))
                return g.tensor_tensor(k_out, ser, la, ALU.add)

            KF, KB = 19, 29

            def chunk_ends(front, back):
                if front is not None:
                    flink = Link(pool, S["front_link"], KF * front, nop=True)
                if back is not None:
                    blink = link = Link(pool, S["back_link"], KB * back, nop=True)
                    pool.wait_ge(S["sq1"], back + 1)
                    pool.nop(nofuse=True)
                    link(g.tensor_scalar(r["n2"], r["m2"], MIN_NORM2, None, ALU.max))
                    link(g.tensor_tensor(r["minv"], r["n2"], NHALF[:, 0:BLK], ALU.pow))
                    link(g.tensor_tensor(r["t"], r["n2"], r["minv"], ALU.mult))
                    g.tensor_tensor(r["q"], r["t"], r["fx"], ALU.mult).then_inc(S["q"], 1)
                    pool.wait_ge(S["tq"], back + 1)
                    pool.nop(nofuse=True)
                    link(g.tensor_scalar(r["tq"], r["tq"], MAX_NORM, None, ALU.min))
                    link(g.tensor_tensor(r["rsc"], r["tq"], r["minv"], ALU.mult))
                    link(g.tensor_tensor(r["x2"], r["rsc"], r["rsc"], ALU.mult))
                    link(g.tensor_tensor(r["x2"], r["x2"], r["m2"], ALU.mult))
                    link(g.tensor_tensor(r["xy"], r["rsc"], r["pxy"], ALU.mult))
                    link(g.tensor_scalar(r["xy"], r["xy"], 2.0, 1.0, ALU.mult, ALU.add))
                    link(g.tensor_tensor(r["a"], r["xy"], y2[:, 0:1].to_broadcast([P, BLK]), ALU.add))
                    link(g.tensor_scalar(r["b"], r["x2"], -1.0, 1.0, ALU.mult, ALU.add))
                    link(g.tensor_tensor(r["den"], r["x2"], y2[:, 0:1].to_broadcast([P, BLK]), ALU.mult))
                    link(g.tensor_tensor(r["den"], r["den"], r["xy"], ALU.add))
                    link(g.tensor_scalar(r["den"], r["den"], MIN_NORM, None, ALU.max))
                    link(g.tensor_tensor(r["den"], r["den"], NEG1[:, :], ALU.pow))
                    link(g.tensor_tensor(r["beta"], r["b"], r["den"], ALU.mult))
                    link(g.tensor_tensor(r["a"], r["a"], r["den"], ALU.mult))
                    g.tensor_tensor(r["alpha"], r["a"], r["rsc"], ALU.mult).then_inc(S["alphabeta"], 1)
                if front is not None:
                    pool.wait_ge(S["stats1"], front + 1)
                    pool.nop(nofuse=True)
                    flink(g.tensor_scalar(r["v"], MV[:, :, 1], LN_EPS, None, ALU.add))
                    g.tensor_tensor(r["rs"], r["v"], NHALF[:, 0:BLK], ALU.pow).then_inc(S["rs1"], 1)
                    g.tensor_tensor(v4(XR[:, :]), v4(XR[:, :]), b4(BOUT[:, :]), ALU.add).then_inc(S["xb"], 1)
                if back is not None:
                    pool.wait_ge(S["sq2"], back + 1)
                    pool.nop(nofuse=True)
                    atanh_begin(blink, 2, r["h2"], MAX_NORM, "tc2")
                if back is not None:
                    atanh_end(blink, 2, back, "ln2", r["kap"]).then_inc(S["kap"], 1)
                    assert blink.n == KB, blink.n
                if front is not None:
                    pool.wait_ge(S["stats2"], front + 1)
                    pool.nop(nofuse=True)
                    flink(g.tensor_scalar(r["v"], MV2[:, :, 1], LN_EPS, None, ALU.add))
                    g.tensor_tensor(r["rs2"], r["v"], NHALF[:, 0:BLK], ALU.pow).then_inc(S["rs2"], 1)
                    pool.wait_ge(S["rs2"], front + 1)
                    flink(g.tensor_tensor(r["mm"], MV2[:, :, 0], r["rs2"], ALU.mult))
                    g.tensor_scalar(r["mm"], r["mm"], -1.0, None, ALU.mult).then_inc(S["minus_mean"], 1)
                    flink(g.tensor_tensor(r["sq"], r["rs2"], r["rs2"], ALU.mult))
                    flink(g.tensor_tensor(r["sq"], r["sq"], MV2[:, :, 1], ALU.mult))
                    flink(g.tensor_scalar(r["sq"], r["sq"], float(P), None, ALU.mult))
                    atanh_begin(flink, 1, r["sq"], ATANH_CLIP, "tc1")
                if front is not None:
                    flink(atanh_end(flink, 1, front, "ln1", r["fx"]))
                    pool.wait_ge(S["x1_ready"], front + 1)
                    pool.nop(nofuse=True)
                    pool.dma_start(x1_dram[bass.ds(front * P, P), :], X1[:, :]).then_inc(S["x1_stored"], 16)
                    pool.wait_ge(S["x1_stored"], 16 * (front + 1))
                    assert flink.n == KF, flink.n

            KR = 10

            def reload(e):
                pool.dma_start(XR[:, :], x1_dram[bass.ds(e * P, P), :]).then_inc(S["x1_back"], 16)

            def result1(e):
                link = Link(pool, S["result_link"], KR * e, nop=True)
                pool.wait_ge(S["sq3"], e + 1)
                pool.nop(nofuse=True)
                link(g.tensor_scalar(r["s2"], r["s2"], MIN_NORM2, None, ALU.max))
                link(g.tensor_tensor(r["w"], r["s2"], NHALF[:, 0:BLK], ALU.pow))
                link(g.tensor_scalar(r["w"], r["w"], ATANH_MAX_NORM, None, ALU.mult))
                link(g.tensor_scalar(r["w"], r["w"], 1.0, None, ALU.min))
                link(g.tensor_scalar(r["r2"], r["r2"], MIN_NORM2, None, ALU.max))
                link(g.tensor_tensor(r["nr"], r["r2"], NHALF[:, 0:BLK], ALU.pow))
                link(g.tensor_tensor(r["nr"], r["nr"], r["r2"], ALU.mult))
                link(g.tensor_tensor(r["nr"], r["nr"], r["w"], ALU.mult))
                g.tensor_scalar(r["t"], r["nr"], MIN_NORM, None, ALU.max).then_inc(S["n3"], 1)
                pool.wait_ge(S["n3"], e + 1)
                link(g.tensor_tensor(r["cf"], r["t"], NEG1[:, :], ALU.pow))
                pool.wait_ge(S["th3"], e + 1)
                pool.nop(nofuse=True)
                link(g.tensor_scalar(r["thn"], r["thn"], MAX_NORM, None, ALU.min))
                g.tensor_tensor(r["cf"], r["cf"], r["thn"], ALU.mult).then_inc(S["coef"], 1)
                pool.wait_ge(S["coef"], 2 * e + 1)
                g.tensor_tensor(r["coef"], r["cf"], r["w"], ALU.mult).then_inc(S["coef"], 1)
                assert link.n == KR, link.n

            def result2(e):
                pool.wait_ge(S["stats3"], e + 1)
                pool.nop(nofuse=True)
                g.tensor_scalar(r["v"], MV[:, :, 1], LN_EPS, None, ALU.add).then_inc(S["rs3"], 1)
                pool.wait_ge(S["rs3"], 2 * e + 1)
                g.tensor_tensor(r["rs"], r["v"], NHALF[:, 0:BLK], ALU.pow).then_inc(S["rs3"], 1)

            def store(e):
                pool.wait_ge(S["res"], e + 1)
                pool.nop(nofuse=True)
                pool.dma_start(out[bass.ds(e * P, P), :], X1[:, :]).then_inc(S["res_stored"], 16)

            def stored(e):
                pool.wait_ge(S["res_stored"], 16 * (e + 1))

            pool.wait_ge(S["y2_ready"], 1)
            chunk_ends(0, None)
            with pool.Fori(2, NCH + 1) as c:
                chunk_ends(c - 1, c - 2)
            chunk_ends(None, NCH - 1)
            reload(0)
            result1(0)
            with pool.Fori(1, NCH) as e:
                result2(e - 1)
                reload(e)
                store(e - 1)
                result1(e)
                stored(e - 1)
            result2(NCH - 1)
            store(NCH - 1)
            stored(NCH - 1)

        @block.scalar
        def _(act):
            a = nc.scalar
            r = {k: v[:, :] for k, v in small.items()}
            act.wait_ge(S["gum1"], 1)
            a.activation(U[:, :], U[:, :], ACT.Ln).then_inc(S["gum2"], 1)
            act.wait_ge(S["gum1"], 2)
            a.activation(U[:, :], U[:, :], ACT.Ln).then_inc(S["gum2"], 1)

            def scale(q, side, i):
                k = par(side, i)
                act.wait_ge(S["pre_rs"], q + 1)
                act.wait_ge(S["pre_z"], q + 1)
                for t in range(BLK):
                    last = a.activation(ROWS[i][:, blk(t)], ROWS[i][:, blk(t)], ACT.Copy,
                                        scale=small[("rs", "rs2")[k]][:, t:t + 1])
                last.then_inc(S["pre_scaled"], 1)

            def transposed(q, side, i, batch):
                k = par(side, i)
                act.wait_ge(S["pre_tr"], q + 1)
                wait_n(act, f"xnt_stored{k}", 8 * PB * (batch - side) + 16 * ((PB * side + i) // 2))
                if not isinstance(q, int) or q >= 2:
                    act.wait_ge(S["pre_logit"], q - 1)
                a.activation((XNT, X1T)[k][:, :], E[:, 2 * k, :], ACT.Copy).then_inc(S["pre_xt"], 1)

            def main(q0, side, batch, between):
                scale(q0, side, 0)
                for i in range(PB):
                    if i + 1 < PB:
                        scale(q0 + i + 1, side, i + 1)
                        between(i + 1)
                    transposed(q0 + i, side, i, batch)

            def gates(b, side, part):
                rows = bass.ds(b * PB * BLK, PB * BLK)
                if part == 0:
                    return
                if part == 1:
                    act.wait_ge(S["gate_arg"], b + 1)
                    a.activation(LG[:, rows, :], LG[:, rows, :], ACT.Exp).then_inc(S["gate_exp"], 1)
                    return
                for i in range(PB):
                    q = b * PB + i
                    act.wait_ge(S["gated"], q + 1)
                    a.activation(XGH[:, bass.ds(q * CW, CW)], norm_rows(side, i), ACT.Copy).then_inc(S["xgh"], 1)
            prelude(act, main, gates)
            act.wait_ge(S["gate_tr"], 1)
            a.activation(GATET[:, :], E[0:NB, 3, 0:P], ACT.Copy).then_inc(S["gate_rows"], 1)

            def hyp_setup(j):
                if j == HB_SQ:
                    act.wait_ge(S["vecs"], 128)
                    a.activation(JUNK[:, 0:P], HB[:, :], ACT.Square, accum_out=hbs[:, 0:1]).then_inc(S["hb_sq"], 1)
                if j == HB_TANH:
                    act.wait_ge(S["hb_norm"], 1)
                    a.activation(hbs[:, 4:5], hbs[:, 3:4], ACT.Tanh).then_inc(S["hb_tanh"], 1)
                if j == HB_Y2:
                    act.wait_ge(S["hb_ready"], 1)
                    a.activation(JUNK[:, 0:P], HB[:, :], ACT.Square, accum_out=y2[:, 0:1]).then_inc(S["y2_ready"], 1)
                if j == HB_OUT:
                    act.wait_ge(S["rm_psum"], 1)
                    a.activation(RM[:, :], E[:, 3, 0:P + 1], ACT.Copy).then_inc(S["rm_ready"], 1)

            def split_high(step, j, k, h):
                if h == 0:
                    turns = (step.n0 + k - k % RING) // RING if isinstance(step.n0, int) else (step.n0 >> 2) + k // RING
                    act.wait_ge(S[f"ld{k % RING}"], 16 * (turns + 1))
                n = 2 * step.n0 + j
                if not (isinstance(n, int) and n < SPLITS):
                    act.wait_ge(S["used"], n - SPLITS + 1)
                a.activation(AH[:, j % SPLITS, :], A[:, k % RING, h * HW:(h + 1) * HW], ACT.Copy).then_inc(S["hi"], 1)

            def lns(k, e, tc_sem, ln_sem):
                act.wait_ge(S[tc_sem], e + 1)
                a.activation(r[f"la_{k}"], r[f"tc_{k}"], ACT.Ln, bias=1.0, scale=1.0)
                a.activation(r[f"lb_{k}"], r[f"tc_{k}"], ACT.Ln, bias=1.0, scale=-1.0).then_inc(S[ln_sem], 1)

            def chunk_ends(j, front, back):
                if j == MX_OUT and back is not None:
                    act.wait_ge(S["mx"], back + 1)
                    a.activation(v4(HY[:, :]), E[:, :, 0:P], ACT.Copy)
                    for t in range(BLK):
                        a.activation(JUNK[:, blk(t)], E[:, t, 0:P], ACT.Square, accum_out=small["m2"][:, t:t + 1])
                    a.activation(r["pxy"], E[:, :, P], ACT.Copy).then_inc(S["sq1"], 1)
                if j == TQ and back is not None:
                    act.wait_ge(S["q"], back + 1)
                    a.activation(r["tq"], r["q"], ACT.Tanh).then_inc(S["tq"], 1)
                if j == TANH and front is not None:
                    act.wait_ge(S["l0_mm"], front + 1)
                    a.activation(v4(TH[:, :]), E[:, :, 0:P], ACT.Tanh, scale=0.5).then_inc(S["tanh"], 1)
                if j == SCALE and back is not None:
                    act.wait_ge(S["alphabeta"], back + 1)
                    for t in range(BLK):
                        a.activation(HY[:, blk(t)], HY[:, blk(t)], ACT.Copy,
                                     scale=small["alpha"][:, t:t + 1]).then_inc(S["scaled"], 1)
                if j == SQ2 and back is not None:
                    act.wait_ge(S["h"], back + 1)
                    for t in range(BLK):
                        last = a.activation(JUNK[:, blk(t)], HY[:, blk(t)], ACT.Square, accum_out=small["h2"][:, t:t + 1])
                    last.then_inc(S["sq2"], 1)
                if j == LN2 and back is not None:
                    lns(2, back, "tc2", "ln2")
                if j == LN1 and front is not None:
                    lns(1, front, "tc1", "ln1")
                if j == XT and back is not None:
                    act.wait_ge(S["kap"], back + 1)
                    for t in range(BLK):
                        a.activation(XTH[:, bass.ds(back * CW + t * P, P)], HY[:, blk(t)], ACT.Copy,
                                     scale=small["kap"][:, t:t + 1]).then_inc(S["xth"], 1)
                if j == X1_AT and front is not None:
                    act.wait_ge(S["minus_mean"], front + 1)
                    for t in range(BLK):
                        last = a.activation(X1[:, blk(t)], FU[:, blk(t)], ACT.Identity, bias=small["mm"][:, t:t + 1],
                                            scale=small["rs2"][:, t:t + 1])
                    last.then_inc(S["x1_ready"], 1)
                if j == X1T_AT and front is not None:
                    act.wait_ge(S["x1_tr"], front + 1)
                    a.activation(X1T[:, :], E[:, 0, :], ACT.Copy).then_inc(S["x1t"], 1)

            def result(event, e):
                if event == "relu":
                    act.wait_ge(S["s2_tr"], e + 1)
                    wait_n(act, "stats3", e)
                    a.activation(TH[:, :], E[:, 0, :], ACT.Relu).then_inc(S["act_link"], 1)
                    for t in range(BLK):
                        a.activation(JUNK[:, blk(t)], E[:, 0, blk(t)], ACT.Square, accum_out=small["s2"][:, t:t + 1])
                    act.wait_ge(S["act_link"], e + 1)
                    for t in range(BLK):
                        last = a.activation(X1T[:, blk(t)], TH[:, blk(t)], ACT.Square, accum_out=small["r2"][:, t:t + 1])
                    last.then_inc(S["sq3"], 1)
                if event == "tanh":
                    act.wait_ge(S["n3"], e + 1)
                    a.activation(r["thn"], r["t"], ACT.Tanh).then_inc(S["th3"], 1)

            def body(step):
                for j, k, h, d, q in step.halves():
                    split_high(step, j, k, h)
                    if step.first:
                        hyp_setup(j)
                    chunk_ends(j, step.front, step.back)
                    for event, e, _ in results(step, j):
                        result(event, e)
            steps(act, body)
            for event, e in tail():
                result(event, e)

        @block.vector
        def _(dve):
            v = nc.vector
            r = {k: t[:, :] for k, t in small.items()}
            link = Link(dve, S["dve_link"])
            dve.wait_ge(S["urow"], 16)
            v.tensor_scalar(U[:, :], U[:, :], U_EPS, 1.0, ALU.max, ALU.min).then_inc(S["gum1"], 1)
            dve.wait_ge(S["gum2"], 1)
            v.tensor_scalar(U[:, :], U[:, :], -1.0, U_EPS, ALU.mult, ALU.add).then_inc(S["gum1"], 1)
            def stats(src, mv, done):
                for t in range(BLK):
                    last = v.bn_stats(BS[:, t, :], src[:, blk(t)])
                link(last)
                dve.nop(nofuse=True)
                for t in range(BLK):
                    last = v.bn_aggr(mv[:, t, :], BS[:, t, :])
                last.then_inc(S[done], 1)

            DONE = 6

            dve.wait_ge(S["norm_vecs"], 32)

            def main(q0, side, batch, between):
                nonlocal link
                for i in range(PB):
                    q, k, buf = q0 + i, par(side, i), (XR, FU, GB)[i]
                    link = Link(dve, S["stats_link"], q)
                    dve.wait_ge(S[f"xin{i}"], 16 * (batch + 1))
                    if not isinstance(q, int) or q >= 2:
                        dve.wait_ge(S["pre_rs"], q - 1)
                    if not isinstance(q, int) or q >= PB:
                        dve.wait_ge(S["pre_xn"], q - PB + 1)
                    stats(buf, (MV, MV2)[k], "pre_stats")
                    dve.wait_ge(S["pre_stats"], q + 1)
                    for t in range(BLK):
                        last = v.scalar_tensor_tensor(out=ROWS[i][:, blk(t)], in0=buf[:, blk(t)],
                                                      scalar=(MV, MV2)[k][:, t, 0:1], in1=GIN[:, :],
                                                      op0=ALU.subtract, op1=ALU.mult)
                    last.then_inc(S["pre_z"], 1)
                    between(i)

            KG = 7

            def gates(b, side, part):
                if part == 0:
                    return low_parts(b, side)
                link = Link(dve, S["gate_link"], KG * b + 3 * (part - 1))
                rows, cols = bass.ds(b * PB * BLK, PB * BLK), bass.ds(b * PB * BLK * 2, PB * BLK * 2)
                if part == 2:
                    return gates_end(b, side, link, rows)
                dve.wait_ge(S["gum2"], 2)
                dve.wait_ge(S["vecs"], 128)
                dve.wait_ge(S["pre_logit"], PB * (b + 1))
                link(v.scalar_tensor_tensor(out=LG[:, rows, :].rearrange("p b k -> p (b k)"), in0=U[:, cols],
                                            scalar=-1.0, in1=E[:, 1 + 2 * side, cols], op0=ALU.mult, op1=ALU.add))
                link(v.tensor_tensor(LG[:, rows, :], LG[:, rows, :], BNB[:, :].rearrange("p (o k) -> p o k", o=1)
                                     .to_broadcast([P, PB * BLK, 2]), ALU.add))
                link(v.tensor_tensor(TOP[:, rows], LG[:, rows, 0], LG[:, rows, 1], ALU.max))
                v.tensor_tensor(LG[:, rows, 0], LG[:, rows, 0], TOP[:, rows], ALU.subtract)
                v.tensor_tensor(LG[:, rows, 1], LG[:, rows, 1], TOP[:, rows], ALU.subtract).then_inc(S["gate_arg"], 1)
                assert link.n == 3

            def gates_end(b, side, link, rows):
                dve.wait_ge(S["gate_exp"], b + 1)
                link(v.tensor_tensor(SM[:, rows], LG[:, rows, 0], LG[:, rows, 1], ALU.add))
                link(v.reciprocal(SM[:, rows], SM[:, rows]))
                v.tensor_tensor(LG[:, rows, 0], LG[:, rows, 0], SM[:, rows], ALU.mult)
                link(v.tensor_tensor(LG[:, rows, 1], LG[:, rows, 1], SM[:, rows], ALU.mult))
                v.tensor_tensor(TOP[:, rows], LG[:, rows, 1], LG[:, rows, 0], ALU.is_gt).then_inc(S["gate_hard"], 1)
                dve.wait_ge(S["gate_hard"], b + 1)
                link(v.tensor_tensor(TOP[:, rows], TOP[:, rows], LG[:, rows, 1], ALU.add))
                v.tensor_tensor(GATE[:, rows], TOP[:, rows], LG[:, rows, 1], ALU.subtract).then_inc(S["gates"], 1)
                dve.wait_ge(S["gates"], b + 1)
                for i in range(PB):
                    q = b * PB + i
                    x4 = v4(norm_rows(side, i))
                    v.tensor_tensor(x4, x4, GATE[:, bass.ds(q * BLK, BLK)].rearrange("p (b o) -> p b o", o=1)
                                    .to_broadcast([P, BLK, P]), ALU.mult).then_inc(S["gated"], 1)
                assert link.n == KG - 3, link.n

            def low_parts(b, side):
                for i in range(PB):
                    q = b * PB + i
                    cols = bass.ds(q * CW, CW)
                    dve.wait_ge(S["xgh"], q + 1)
                    v.tensor_tensor(XGL[:, cols], norm_rows(side, i), XGH[:, cols].bitcast(F32),
                                    ALU.subtract).then_inc(S["xgl"], 1)
            prelude(dve, main, gates)
            link = Link(dve, S["dve_link"])
            def prepare():
                dve.wait_ge(S["weights"], 16 * 7)
                v.tensor_scalar(RX[:, P:2 * P], RX[:, P:2 * P], 0.5, None, ALU.mult)
                v.tensor_scalar(RS[:, P:2 * P], RS[:, P:2 * P], -0.5, None, ALU.mult).then_inc(S["wt_scaled"], 1)
                dve.wait_ge(S["vecs"], 128)
                dve.wait_ge(S["const"], 1)
                link(v.tensor_tensor(B3[:, P:2 * P], B3[:, P:2 * P], B3[:, 2 * P:3 * P], ALU.subtract))
                link(v.tensor_scalar(B3[:, P:2 * P], B3[:, P:2 * P], 0.5, None, ALU.mult))
                for row in (0, 32):
                    v.tensor_copy(BP[row:row + 1, :], B3[row:row + 1, :])
                    link(v.tensor_copy(BR[:, :], B3[:, :]))
                    link(v.tensor_tensor(B3[:, :], B3[:, :], BR[:, :], ALU.subtract))
                v.tensor_copy(BP[64:65, :], B3[64:65, :]).then_inc(S["bias_ready"], 1)
                if first_low < NCH:
                    v.memset(PART[:, 0, :], 0.0)
                assert link.n == DONE

            def split_low(step, j, k, h):
                dve.wait_ge(S["hi"], 2 * step.n0 + j + 1)
                v.tensor_tensor(AL[:, j % SPLITS, :], A[:, k % RING, h * HW:(h + 1) * HW],
                                AH[:, j % SPLITS, :].bitcast(F32), ALU.subtract).then_inc(S["lo"], 1)

            K1 = 6

            def chunk_ends(j, front, back, complete):
                if j == GATED and front is not None:
                    dve.wait_ge(S["used"], complete)
                    dve.wait_ge(S["epi_in"], 48 * (front + 1))
                    v.tensor_tensor(GB[:, :], ACC[:, bass.ds((front % 2) * CW, CW)], GB[:, :],
                                    ALU.mult).then_inc(S["s1_gated"], 1)
                if j == FUSE and front is not None:
                    dve.wait_ge(S["tanh"], front + 1)
                    link(v.scalar_tensor_tensor(out=v4(FU[:, :]), in0=v4(TH[:, :]), scalar=1.0,
                                                in1=E[:, :, P:2 * P], op0=ALU.add, op1=ALU.mult))
                    link(v.tensor_tensor(v4(FU[:, :]), v4(FU[:, :]), E[:, :, 2 * P:3 * P], ALU.add))
                    link(v.tensor_tensor(FU[:, :], FU[:, :], XR[:, :], ALU.add))
                if j == STATS1 and front is not None:
                    stats(FU, MV, "stats1")
                if j == H_AT and back is not None:
                    for t in range(BLK):
                        dve.wait_ge(S["scaled"], BLK * back + t + 1)
                        last = v.scalar_tensor_tensor(out=HY[:, blk(t)], in0=HB[:, :],
                                                      scalar=small["beta"][:, t:t + 1], in1=HY[:, blk(t)],
                                                      op0=ALU.mult, op1=ALU.add)
                    last.then_inc(S["h"], 1)
                if j == CENTER and front is not None:
                    dve.wait_ge(S["rs1"], front + 1)
                    for t in range(BLK):
                        last = v.scalar_tensor_tensor(out=FU[:, blk(t)], in0=FU[:, blk(t)], scalar=MV[:, t, 0:1],
                                                      in1=GOUT[:, :], op0=ALU.subtract, op1=ALU.mult)
                    last.then_inc(S["centered"], 1)
                if j == SHIFT and front is not None:
                    dve.wait_ge(S["centered"], front + 1)
                    dve.wait_ge(S["xb"], front + 1)
                    for t in range(BLK):
                        last = v.scalar_tensor_tensor(out=FU[:, blk(t)], in0=FU[:, blk(t)],
                                                      scalar=small["rs"][:, t:t + 1], in1=XR[:, blk(t)],
                                                      op0=ALU.mult, op1=ALU.add)
                    link(last)
                if j == STATS2 and front is not None:
                    stats(FU, MV2, "stats2")
                if j == XT and back is not None:
                    for t in range(BLK):
                        cols = bass.ds(back * CW + t * P, P)
                        dve.wait_ge(S["xth"], BLK * back + t + 1)
                        last = v.scalar_tensor_tensor(out=XTL[:, cols], in0=HY[:, blk(t)],
                                                      scalar=small["kap"][:, t:t + 1], in1=XTH[:, cols].bitcast(F32),
                                                      op0=ALU.mult, op1=ALU.subtract)
                    last.then_inc(S["xtl"], 1)

            K3, STATS_LINKS = 2, NCH

            def result(event, e, complete, with_part):
                nonlocal link
                if event == "take":
                    dve.wait_ge(S["used"], complete)
                    wait_n(dve, "s2_tr", e)
                    acc = ACC[:, bass.ds((e % 4) * CW, CW)]
                    if with_part:
                        v.tensor_tensor(GB[:, :], acc, PART[:, e - (first_low - 1), :], ALU.add).then_inc(S["s2_taken"], 1)
                    else:
                        v.tensor_copy(GB[:, :], acc).then_inc(S["s2_taken"], 1)
                if event == "add":
                    link = Link(dve, S["stats_link"], STATS_LINKS + K3 * e)
                    dve.wait_ge(S["coef"], 2 * e + 2)
                    dve.wait_ge(S["x1_back"], 16 * (e + 1))
                    for t in range(BLK):
                        last = v.scalar_tensor_tensor(out=FU[:, blk(t)], in0=TH[:, blk(t)],
                                                      scalar=small["coef"][:, t:t + 1], in1=XR[:, blk(t)],
                                                      op0=ALU.mult, op1=ALU.add)
                    link(last)
                    stats(FU, MV, "stats3")
                    assert link.n == K3
                if event == "norm":
                    dve.wait_ge(S["rs3"], 2 * e + 2)
                    for t in range(BLK):
                        last = v.tensor_scalar(X1[:, blk(t)], FU[:, blk(t)], MV[:, t, 0:1],
                                               small["rs"][:, t:t + 1], ALU.subtract, ALU.mult)
                    last.then_inc(S["res"], 1)

            def body(step):
                nonlocal link
                if step.front is not None:
                    link = Link(dve, S["dve_link"], DONE + K1 * step.front)
                for j, k, h, d, q in step.halves():
                    split_low(step, j, k, h)
                    if step.first and j == PREPARE:
                        prepare()
                    if step.phase == 1 and step.lw and j == min(2 * (both_from(step.lw) + step.lw) + SPLITS - 1, 2 * NCH - 1):
                        dve.wait_ge(S["used"], 2 * (step.n0 + both_from(step.lw) + step.lw))
                        v.tensor_copy(PART[:, step.c - (first_low - 1), :],
                                      ACC[:, bass.ds((step.c % 2) * CW + 2 * CW, CW)]).then_inc(S["part_saved"], 1)
                    chunk_ends(j, step.front, step.back, 2 * step.n0)
                    for event, e, complete in results(step, j):
                        result(event, e, complete, step.lw > 0)
                if step.front is not None:
                    assert link.n == K1, link.n
            steps(dve, body)
            for event, e in tail():
                result(event, e, 2 * TOTAL, True)

        @block.tensor
        def _(pe):
            p = nc.tensor
            pe.wait_ge(S["weights"], 16 * 7)
            pe.wait_ge(S["ident_ready"], 2)
            def transposes(q, side, i):
                pe.wait_ge(S["pre_xn"], q + 1)
                if not isinstance(q, int) or q >= 2:
                    pe.wait_ge(S["pre_xt"], q - 1)
                for t in range(BLK):
                    last = p.transpose(E[:, 2 * par(side, i), blk(t)], norm_rows(side, i)[:, blk(t)], ident[:, :])
                last.then_inc(S["pre_tr"], 1)

            def logits(q, side, i):
                xt = (XNT, X1T)[par(side, i)]
                pe.wait_ge(S["pre_xt"], q + 1)
                for t in range(BLK):
                    last = p.matmul(E[:, 1 + 2 * side, bass.ds(q * 2 * BLK + 2 * t, 2)], xt[:, blk(t)], WN[:, :],
                                    start=True, stop=True)
                last.then_inc(S["pre_logit"], 1)

            def main(q0, side, batch, between):
                transposes(q0, side, 0)
                if not isinstance(batch, int) or batch >= 2:
                    pe.wait_ge(S["gate_arg"], batch - 1)
                for i in range(PB):
                    if i + 1 < PB:
                        transposes(q0 + i + 1, side, i + 1)
                    logits(q0 + i, side, i)
            prelude(pe, main)
            pe.wait_ge(S["gates"], NCH // PB)
            p.transpose(E[0:NB, 3, 0:P], GATE[:, :], ident[:, :]).then_inc(S["gate_tr"], 1)

            def chunk_ends(j, front, back):
                if front is not None and L0 <= j < L0 + BLK * L0_EVERY and (j - L0) % L0_EVERY == 0:
                    if j == L0:
                        pe.wait_ge(S["s1_gated"], front + 1)
                        pe.wait_ge(S["epi_in"], 48 * (front + 1))
                        if back is not None:
                            pe.wait_ge(S["sq1"], back + 1)
                    t = (j - L0) // L0_EVERY
                    p.matmul(E[:, t, 0:3 * P], ones[:, :], BP[:, :], start=True, stop=False)
                    p.matmul(E[:, t, 0:2 * P], XNT[:, blk(t)], RX[:, :], start=False, stop=False)
                    last = p.matmul(E[:, t, 0:3 * P], GB[:, blk(t)], RS[:, :], start=False, stop=True)
                    if t == BLK - 1:
                        last.then_inc(S["l0_mm"], 1)
                if front is not None and j == X1_TR:
                    pe.wait_ge(S["x1_ready"], front + 1)
                    for t in range(BLK):
                        last = p.transpose(E[:, 0, blk(t)], X1[:, blk(t)], ident[:, :])
                    last.then_inc(S["x1_tr"], 1)
                if front is not None and j == MX:
                    pe.wait_ge(S["x1t"], front + 1)
                    for t in range(BLK):
                        last = p.matmul(E[:, t, 0:P + 1], X1T[:, blk(t)], RM[:, :], start=True, stop=True)
                    last.then_inc(S["mx"], 1)

            def three_pass(acc, hi, lo, q, t, j, start, stop):
                st = blk(BLK * q + t)
                mv = slice((t % 2) * CW, (t % 2 + 1) * CW)
                p.matmul(acc, hi[:, st], AH[:, j % SPLITS, mv], start=start, stop=False)
                p.matmul(acc, hi[:, st], AL[:, j % SPLITS, mv], start=False, stop=False)
                return p.matmul(acc, lo[:, st], AH[:, j % SPLITS, mv], start=False, stop=stop)

            def result(event, e):
                if event == "turn":
                    pe.wait_ge(S["s2_taken"], e + 1)
                    wait_n(pe, "sq3", e)
                    for t in range(BLK):
                        last = p.transpose(E[:, 0, blk(t)], GB[:, blk(t)], ident[:, :])
                    last.then_inc(S["s2_tr"], 1)

            def body(step):
                c, lw = step.c, step.lw
                for j, k, h, d, q in step.halves():
                    if step.phase == 1 and isinstance(c, int) and c == 0 and h == 0:
                        pe.wait_ge(S["xgl"], q + 1)
                    if step.phase == 1 and q < lw and h == 0:
                        pe.wait_ge(S["xtl"], q + 1)
                    if step.mixed:
                        if h == 0:
                            pe.wait_ge(S["xtl"], q + 1)
                        if q == 0 and h == 0 and d < 2:
                            pe.wait_ge(S["s1_gated"], NCH - 1 + d)
                        if q == 0 and h == 0 and d == 2 and first_low < NCH:
                            pe.wait_ge(S["part_saved"], NCH - first_low)
                    pe.wait_ge(S["lo"], 2 * step.n0 + j + 1)
                    for t in (2 * h, 2 * h + 1):
                        if step.phase == 1:
                            last = three_pass(ACC[:, bass.ds((c % 2) * CW, CW)], XGH, XGL, q, t, j,
                                              k == 0 and t == 0, k == NCH - 1 and t == BLK - 1)
                            if q < lw:
                                last = three_pass(ACC[:, bass.ds((c % 2) * CW + 2 * CW, CW)], XTH, XTL, q, t, j, q == 0 and t == 0,
                                                  q == lw - 1 and t == BLK - 1)
                        else:
                            last = three_pass(ACC[:, bass.ds(((c + d) % 4) * CW, CW)], XTH, XTL, q, t, j,
                                              q == lw and t == 0, q == NCH - 1 and t == BLK - 1)
                    last.then_inc(S["used"], 1)
                    if step.first and j == HB_MM:
                        pe.wait_ge(S["hb_ready"], 1)
                        pe.wait_ge(S["gate_rows"], 1)
                        p.transpose(E[:, 3, 0:P], WH[:, :], ident[:, :])
                        p.matmul(E[:, 3, P:P + 1], WH[:, :], HBC[:, :], start=True, stop=True).then_inc(S["rm_psum"], 1)
                    if step.first and j == HB_DONE:
                        pe.wait_ge(S["rm_ready"], 1)
                        pe.wait_ge(S["wt_scaled"], 1)
                        pe.wait_ge(S["bias_ready"], 1)
                    chunk_ends(j, step.front, step.back)
                    for event, e, _ in results(step, j):
                        result(event, e)
            steps(pe, body)
            for event, e in tail():
                result(event, e)


_INS = ["x", "adjT", "u", "w1", "b1", "w2", "b2", "wg", "bg", "wn", "bn", "g_in", "b_in", "g_out", "b_out",
        "w_hyp", "b_hyp"]


def kernel(**inputs):
    import numpy as np
    import concourse.bacc as bacc
    from concourse.bass_utils import run_bass_kernel_spmd as run

    given = {k: np.asarray(v) for k, v in inputs.items()}
    n, d = given["x"].shape
    nch = n // CW
    host = {
        "x": given["x"].reshape(nch, BLK, P, d).transpose(0, 2, 1, 3).reshape(nch * P, CW),
        "adjT": given["adj"].reshape(nch, CW, nch, BLK, P).transpose(0, 2, 4, 3, 1).reshape(nch * nch * P, GW),
        "u": given["L0_gnn_u"].reshape(n // P, P, 2).transpose(1, 0, 2).reshape(P, n // P * 2),
        "w1": given["L0_gnn_W1"], "b1": given["L0_gnn_b1"], "w2": given["L0_gnn_W2"], "b2": given["L0_gnn_b2"],
        "wg": given["L0_gnn_Wg"], "bg": given["L0_gnn_bg"], "wn": given["L0_gnn_Wn"], "bn": given["L0_gnn_bn"],
        "g_in": given["L0_gnn_g_in"], "b_in": given["L0_gnn_b_in"], "g_out": given["L0_gnn_g_out"],
        "b_out": given["L0_gnn_b_out"], "w_hyp": given["L1_gnn_weight"], "b_hyp": given["L1_gnn_bias"],
    }
    nc = bacc.Bacc("TRN2", target_bir_lowering=False, num_devices=1)
    arrays, args = {}, []
    for name in _INS:
        a = np.ascontiguousarray(host[name])
        arrays[f"in_{name}_dram"] = a
        args.append(nc.dram_tensor(f"in_{name}_dram", a.shape, mybir.dt.from_np(a.dtype), kind="ExternalInput").ap())
    args.append(nc.dram_tensor("out_0_dram", (nch * P, CW), F32, kind="ExternalOutput").ap())
    build(nc, *args)
    r = run(nc, [arrays], core_ids=[0])
    got = r.results[0]["out_0_dram"]
    return got.reshape(nch, P, BLK, d).transpose(0, 2, 1, 3).reshape(n, d)
```
